# Optimizing a Trainium2 kernel written in Bass

```python
import numpy as np
import jax
import jax.numpy as jnp

def _softmax(x, axis=-1):
    return jax.nn.softmax(x, axis=axis)

def _gelu(x):
    return jax.nn.gelu(x, approximate=True)

def _silu(x):
    return jax.nn.silu(x)

def _sigmoid(x):
    return jax.nn.sigmoid(x)

def _layernorm(x, axis=-1, eps=1e-05):
    m = jnp.mean(x, axis=axis, keepdims=True)
    v = jnp.var(x, axis=axis, keepdims=True)
    return (x - m) / jnp.sqrt(v + eps)

def _scatter_add(tgt, idx, src, axis=0):
    return tgt.at[idx].add(src)

def _segment_sum(src, seg, n):
    return jax.ops.segment_sum(src, seg, n)
kernel_name = 'mk_gnn_preln_d4_gnn_r64_9f18d2'

def setup_inputs(seed: int=0):
    np.random.seed(seed)
    _w = jnp.asarray

    def _rec_inputs():
        import jax
        import jax.numpy as jnp
        _gk = jax.random.key(seed)
        x = -0.0009044 + 1 * jax.random.normal(jax.random.fold_in(_gk, 1), (100000, 32), jnp.float32)
        src = jax.random.randint(jax.random.fold_in(_gk, 2), (50000,), 0, 100000, jnp.int32)
        dst = jnp.minimum((100000 * jax.random.uniform(jax.random.fold_in(_gk, 3), (50000,)) ** 2.0).astype(jnp.int32), 99999)
        _o = jnp.argsort(dst, stable=True)
        src = src[_o]
        dst = dst[_o]
        edge_attr_2 = -5.09086e-05 + 0.577461 * jax.random.normal(jax.random.fold_in(_gk, 12), (50000, 2), jnp.float32)
        return (x, src, dst, edge_attr_2)
    x, src, dst, edge_attr_2 = _rec_inputs()

    def _L0_gnn_setup():
        import jax, jax.numpy as jnp
        import numpy as np
        N_NODES = 50000
        N_EDGES = 25000
        F_IN = 32
        F_OUT = 32
        BASIS = (4, 4)

        def _tent_basis(u, n):
            centers = jnp.linspace(-1.0, 1.0, n, dtype=u.dtype)
            h = 2.0 / (n - 1)
            return jnp.maximum(0.0, 1.0 - jnp.abs(u[:, None] - centers[None, :]) / h)
        key = jax.random.key(seed)
        k1, k2, k3, k4, k5 = jax.random.split(key, 5)
        x = jax.random.normal(k1, (N_NODES, F_IN), dtype=jnp.float32)
        edge_attr = jax.random.uniform(k2, (N_EDGES, 2), dtype=jnp.float32, minval=-1.0, maxval=1.0)
        weight = jax.random.uniform(k3, (*BASIS, F_IN, F_OUT), dtype=jnp.float32, minval=-0.05, maxval=0.05)
        src = jax.random.randint(k4, (N_EDGES,), 0, N_NODES)
        tgt = jax.random.randint(k5, (N_EDGES,), 0, N_NODES)
        edge_index = jnp.stack([tgt, src], axis=0).astype(jnp.int64)
        return {'x': x, 'edge_attr': edge_attr, 'weight': weight, 'edge_index': edge_index}
    _L0_gnn_all = _L0_gnn_setup()
    _L0_gnn_in = {k: v for k, v in _L0_gnn_all.items() if k in ('weight',)}
    del _L0_gnn_all

    def _L1_gnn_setup():
        import jax, jax.numpy as jnp
        import numpy as np
        N_NODES = 100000
        N_EDGES = 25000
        NUM_FEATURES = 32
        HIDDEN = 64

        def _gcn_conv(h, W, b, src, dst, norm, inv_deg, n_nodes):
            h = h @ W
            msg = h[src] * norm[:, None]
            agg = jax.ops.segment_sum(msg, dst, num_segments=n_nodes)
            agg = agg + h * inv_deg[:, None]
            return agg + b
        key = jax.random.key(seed)
        k_x, k_e, k_w1, k_b1, k_w2, k_b2 = jax.random.split(key, 6)
        X = jax.random.normal(k_x, (N_NODES, NUM_FEATURES), dtype=jnp.float32)
        connections = jax.random.randint(k_e, (2, N_EDGES), 0, N_NODES, dtype=jnp.int64)
        W1 = jax.random.normal(k_w1, (NUM_FEATURES, HIDDEN), dtype=jnp.float32) / np.sqrt(NUM_FEATURES)
        b1 = jnp.zeros((HIDDEN,), dtype=jnp.float32)
        W2 = jax.random.normal(k_w2, (HIDDEN, NUM_FEATURES), dtype=jnp.float32) / np.sqrt(HIDDEN)
        b2 = jnp.zeros((NUM_FEATURES,), dtype=jnp.float32)
        return {'X': X, 'connections': connections, 'W1': W1, 'b1': b1, 'W2': W2, 'b2': b2}
    _L1_gnn_all = _L1_gnn_setup()
    _L1_gnn_in = {k: v for k, v in _L1_gnn_all.items() if k in ('W1', 'b1', 'W2', 'b2')}
    del _L1_gnn_all

    def _L2_gnn_setup():
        import jax, jax.numpy as jnp
        import numpy as np
        N = 100000
        E = 25000
        F_IN = 32
        F_OUT = 32
        key = jax.random.key(seed)
        k1, k2, k3, k4, k5 = jax.random.split(key, 5)
        x = jax.random.normal(k1, (N, F_IN), dtype=jnp.float32)
        edge_src = jax.random.randint(k2, (E,), 0, N, dtype=jnp.int32)
        edge_dst = jax.random.randint(k3, (E,), 0, N, dtype=jnp.int32)
        bound = 1.0 / np.sqrt(2 * F_IN)
        W = jax.random.uniform(k4, (2 * F_IN, F_OUT), minval=-bound, maxval=bound, dtype=jnp.float32)
        b = jax.random.uniform(k5, (F_OUT,), minval=-bound, maxval=bound, dtype=jnp.float32)
        return {'x': x, 'W': W, 'b': b, 'edge_src': edge_src, 'edge_dst': edge_dst}
    _L2_gnn_all = _L2_gnn_setup()
    _L2_gnn_in = {k: v for k, v in _L2_gnn_all.items() if k in ('W', 'b')}
    del _L2_gnn_all

    def _L3_gnn_setup():
        import jax, jax.numpy as jnp
        import numpy as np
        N_NODES = 100000
        N_EDGES = 25000
        D_FEAT = 32
        K = 10
        ALPHA = 0.1
        key = jax.random.key(seed)
        k1, k2, k3 = jax.random.split(key, 3)
        feat = jax.random.normal(k1, (N_NODES, D_FEAT), dtype=jnp.float32)
        src = jax.random.randint(k2, (N_EDGES,), 0, N_NODES, dtype=jnp.int64)
        dst = jax.random.randint(k3, (N_EDGES,), 0, N_NODES, dtype=jnp.int64)
        return {'feat': feat, 'src': src, 'dst': dst}
    _L3_gnn_all = _L3_gnn_setup()
    _L3_gnn_in = {k: v for k, v in _L3_gnn_all.items() if k in ()}
    del _L3_gnn_all
    return {'x': x, 'src': src, 'dst': dst, 'edge_attr_2': edge_attr_2, 'L0_gnn_weight': _L0_gnn_in['weight'], 'L1_gnn_W1': _L1_gnn_in['W1'], 'L1_gnn_b1': _L1_gnn_in['b1'], 'L1_gnn_W2': _L1_gnn_in['W2'], 'L1_gnn_b2': _L1_gnn_in['b2'], 'L2_gnn_W': _L2_gnn_in['W'], 'L2_gnn_b': _L2_gnn_in['b']}

def reference(x, src, dst, edge_attr_2, L0_gnn_weight, L1_gnn_W1, L1_gnn_b1, L1_gnn_W2, L1_gnn_b2, L2_gnn_W, L2_gnn_b):
    import jax
    import jax.numpy as jnp

    def _L0_gnn_ref(x, edge_attr, weight, edge_index):
        import jax, jax.numpy as jnp
        import numpy as np
        N_NODES = 50000
        N_EDGES = 25000
        F_IN = 32
        F_OUT = 32
        BASIS = (4, 4)

        def _tent_basis(u, n):
            centers = jnp.linspace(-1.0, 1.0, n, dtype=u.dtype)
            h = 2.0 / (n - 1)
            return jnp.maximum(0.0, 1.0 - jnp.abs(u[:, None] - centers[None, :]) / h)
        k1, k2, f_in, f_out = weight.shape
        n_nodes = x.shape[0]
        bu = _tent_basis(edge_attr[:, 0], k1)
        bv = _tent_basis(edge_attr[:, 1], k2)
        basis = (bu[:, :, None] * bv[:, None, :]).reshape(-1, k1 * k2)
        xj = x[edge_index[1]]
        w2 = weight.reshape(k1 * k2, f_in, f_out)
        msg = basis[:, 0:1] * (xj @ w2[0])
        for k in range(1, k1 * k2):
            msg = msg + basis[:, k:k + 1] * (xj @ w2[k])
        out = jax.ops.segment_sum(msg, edge_index[0], num_segments=n_nodes)
        return out

    def _L1_gnn_ref(X, connections, W1, b1, W2, b2):
        import jax, jax.numpy as jnp
        import numpy as np
        N_NODES = 100000
        N_EDGES = 25000
        NUM_FEATURES = 32
        HIDDEN = 64

        def _gcn_conv(h, W, b, src, dst, norm, inv_deg, n_nodes):
            h = h @ W
            msg = h[src] * norm[:, None]
            agg = jax.ops.segment_sum(msg, dst, num_segments=n_nodes)
            agg = agg + h * inv_deg[:, None]
            return agg + b
        n_nodes = X.shape[0]
        src, dst = (connections[0], connections[1])
        ones = jnp.ones(src.shape[0], dtype=X.dtype)
        deg = jax.ops.segment_sum(ones, dst, num_segments=n_nodes) + 1.0
        inv_sqrt = jax.lax.rsqrt(deg)
        norm = inv_sqrt[src] * inv_sqrt[dst]
        inv_deg = 1.0 / deg
        h = _gcn_conv(X, W1, b1, src, dst, norm, inv_deg, n_nodes)
        h = _gcn_conv(h, W2, b2, src, dst, norm, inv_deg, n_nodes)
        return jax.nn.relu(h)

    def _L2_gnn_ref(x, W, b, edge_src, edge_dst):
        import jax, jax.numpy as jnp
        import numpy as np
        N = 100000
        E = 25000
        F_IN = 32
        F_OUT = 32
        n = x.shape[0]
        msgs = x[edge_src]
        summed = jax.ops.segment_sum(msgs, edge_dst, num_segments=n)
        cnt = jax.ops.segment_sum(jnp.ones_like(edge_dst, dtype=x.dtype), edge_dst, num_segments=n)
        neigh_mean = summed / jnp.maximum(cnt, 1.0)[:, None]
        h = jnp.concatenate([x, neigh_mean], axis=1)
        return jax.nn.relu(h @ W + b)

    def _L3_gnn_ref(feat, src, dst):
        import jax, jax.numpy as jnp
        import numpy as np
        N_NODES = 100000
        N_EDGES = 25000
        D_FEAT = 32
        K = 10
        ALPHA = 0.1
        n = feat.shape[0]
        ones = jnp.ones(src.shape[0], dtype=feat.dtype)
        out_deg = jax.ops.segment_sum(ones, src, num_segments=n)
        in_deg = jax.ops.segment_sum(ones, dst, num_segments=n)
        src_norm = jnp.clip(out_deg, 1.0, None) ** (-0.5)
        dst_norm = jnp.clip(in_deg, 1.0, None) ** (-0.5)
        feat0 = feat

        def step(f, _):
            f = f * src_norm[:, None]
            agg = jax.ops.segment_sum(f[src], dst, num_segments=n)
            f = agg * dst_norm[:, None]
            f = (1.0 - ALPHA) * f + ALPHA * feat0
            return (f, None)
        feat, _ = jax.lax.scan(step, feat, None, length=K)
        return feat
    edge_index = jnp.stack([src, dst])
    h = jnp.maximum(_layernorm(x, axis=-1), 0.0)
    x = x + _L0_gnn_ref(h, edge_attr_2, L0_gnn_weight, edge_index)
    h = jnp.maximum(_layernorm(x, axis=-1), 0.0)
    x = x + _L1_gnn_ref(h, edge_index, L1_gnn_W1, L1_gnn_b1, L1_gnn_W2, L1_gnn_b2)
    h = jnp.maximum(_layernorm(x, axis=-1), 0.0)
    x = x + _L2_gnn_ref(h, L2_gnn_W, L2_gnn_b, src, dst)
    h = jnp.maximum(_layernorm(x, axis=-1), 0.0)
    x = x + _L3_gnn_ref(h, src, dst)
    return x

_drawn_inputs = setup_inputs


def setup_inputs(seed=0):
    import zlib

    import numpy as np

    out = dict(_drawn_inputs(seed))
    spreads = {'L1_gnn_b1': (0.0, 0.1), 'L1_gnn_b2': (0.0, 0.1)}
    factors = {}
    for name, (base, spread) in spreads.items():
        noise = np.random.default_rng([zlib.crc32(name.encode()), seed]).standard_normal(out[name].shape)
        drawn = base * np.exp(spread * noise) if base else spread * noise
        out[name] = jnp.asarray(drawn.astype(out[name].dtype))
    for name, factor in factors.items():
        out[name] = (out[name] * factor).astype(out[name].dtype)
    return out
```

```python
import concourse.bass as bass
from concourse import mybir
from contextlib import ExitStack

P = 128
CW = 28
F = 32
QW = 4
NQ = CW // QW
TW = F + 1
NW = 36
PASSES = 10
ALPHA = 0.1
EPS = 1e-5


def gnn_stack(nc, x, src, dst, attr, w0, w1, b1, w2, b2, wl, bl, out):
    f32, i32, f16, bf16, u8 = (mybir.dt.float32, mybir.dt.int32, mybir.dt.float16, mybir.dt.bfloat16,
                               mybir.dt.uint8)
    ALU, ACT, AX = mybir.AluOpType, mybir.ActivationFunctionType, mybir.AxisListType

    N, E = x.shape[0], src.shape[0]
    CH = P * CW
    EC = -(-E // (2 * CH)) * 2 * CW
    ECH = EC // CW
    EB = ECH // 2
    NCH = -(-N // (2 * CH)) * 2
    NCOL = NCH * CW
    HW = NCOL // 2
    EP, NP = P * EC, P * NCOL
    ZROW = EP + P
    SRC_PAD, DST_PAD = N + P, N + P + 1
    EFULL, ETAIL = E // EC, E % EC
    NFULL, NREM = N // CH, N % CH
    NPF, NTAIL = NREM // CW, NREM % CW
    SP_N = NCH // EB
    assert NP > DST_PAD and 0 < ETAIL and EFULL < P and HW <= 512 and NFULL == NCH - 1
    assert SP_N * EB == NCH and SP_N % 2 == 0
    ES = CW * F
    GI = 16 * CW

    ctx = ExitStack()
    with ctx:
        def sb(name, shape, dt=f32):
            return ctx.enter_context(nc.sbuf_tensor(name, shape, dt))

        def sem(name):
            return ctx.enter_context(nc.semaphore(name))

        def dram(name, shape):
            return nc.dram_tensor(name, shape, f32, kind="Internal").ap()

        agg0 = [dram(f"agg0_{k}", (NP, TW)) for k in range(QW)]
        nodes = dram("nodes", (NP, NW))
        run1, run2, run3, run4a, run4b = [dram(f"run_{n}", (EP + P + 1, F)) for n in ("1", "2", "3", "4a", "4b")]

        srci = sb("srci", [P, EC], i32)
        dsti = sb("dsti", [P, EC], i32)
        keep = sb("keep", [P, EC + 1])
        start = sb("start", [P, EC])
        keepx = sb("keepx", [P, ECH, ES], u8)
        rowi = sb("rowi", [P, EC], i32)
        outi = sb("outi", [P, EC], i32)
        coefS = sb("coefS", [P, 5, EC])
        coefD = sb("coefD", [P, 5, EC])
        g36 = [sb(f"g36_{b}", [P, CW, NW]) for b in range(2)]
        gbuf = [t[:, :, :].rearrange("p c w -> p (c w)")[:, 0:ES].rearrange("p (c e) -> p c e", e=F) for t in g36]
        ident = sb("ident", [P, P])
        link = sb("link", [P, P])
        bd12, bda, bdb = [sb(n, [P, P]) for n in ("bd12", "bda", "bdb")]
        b12, b12n, b2r, blr = [sb(n, [P, F]) for n in ("b12", "b12n", "b2r", "blr")]
        firstrun, frpart, bound, ends = [sb(n, [P, F]) for n in ("firstrun", "frpart", "bound", "ends")]
        carries = sb("carries", [P, 4, F])
        small = sb("small", [P, 6, CW])
        ii = [sb(f"ii{b}", [P, CW], i32) for b in range(2)]
        di = sb("di", [P, CW], i32)
        epsc = sb("epsc", [P, 1])
        zrow = sb("zrow", [1, F])

        BIGW = 2 * EC * F if EC >= 10 * CW else 26 * EC + 8 * NCOL + 2 * QW * CW * TW + 2 * ES + 2048
        big = sb("big", [P, BIGW])
        work = sb("work", [P, 14 * ES + CW * NW])

        def cutter(region):
            at = [0]

            def cut(n, dt=None):
                v = region[:, at[0]:at[0] + n]
                at[0] += n
                assert at[0] <= region.shape[1], at[0]
                return v.bitcast(dt) if dt is not None else v
            return cut

        def rm(t):
            return t.rearrange("p (c e) -> p c e", e=F)

        xs = rm(big[:, 0:EC * F])
        hs = rm(big[:, EC * F:2 * EC * F])
        xd = xs
        cut = cutter(work)
        mff = cut(ES)
        mf = mff.rearrange("p (f j) -> p f j", j=CW)
        mfr = mff.rearrange("p (f j) -> p j f", j=CW)
        rff = [cut(ES) for _ in range(2)]
        rf = [t.rearrange("p (f j) -> p f j", j=CW) for t in rff]
        ro = [rm(cut(ES)) for _ in range(2)]
        ta, tb, tc = [rm(cut(ES)) for _ in range(3)]
        vT = [cut(ES) for _ in range(2)]
        su = rm(cut(ES))
        sr = [rm(cut(ES)) for _ in range(3)]
        sx = cut(CW * NW).rearrange("p (c w) -> p c w", w=NW)
        lcut = cutter(work)
        lcut(5 * ES)
        lcut(3 * ES)
        same = lcut(QW * P)
        s4 = same.rearrange("p (t q) -> p t q", t=QW)
        s4m = lcut(QW * P).rearrange("p (t q) -> p t q", t=QW)
        hT = [lcut(P) for _ in range(2)]
        ym = work[:, 0:16 * F].rearrange("p (k o) -> p k o", k=16)
        hot = [lcut(HW, bf16) for _ in range(2)]
        hotp = lcut(QW * P // 2, bf16).rearrange("p (t q) -> p t q", t=QW)
        msg = lcut(QW * TW).rearrange("p (t w) -> p t w", w=TW)
        nil = lcut(P // 2, bf16)
        mcut = cutter(work[:, 16 * F:5 * ES])
        ms = [mcut(CW * TW).rearrange("p (c w) -> p c w", w=TW) for _ in range(2)]
        dup = mcut(CW)
        oi = [mcut(CW, i32) for _ in range(2)]
        pad_to = mcut(CW)
        srcc = [mcut(CW) for _ in range(2)]
        bcut = cutter(big)
        basis = bcut(16 * EC).rearrange("p (c k) -> p c k", k=16)
        attr_s = bcut(2 * EC)
        srcf, dstf, wpart, wfree, e1, e2, e3 = [bcut(EC) for _ in range(7)]
        ei = bcut(EC, i32)
        after, before, ones, iotar = [bcut(P) for _ in range(4)]
        iotaw = bcut(NCOL)
        iotan = bcut(HW, f16)
        cuts = bcut(NCOL)
        w0r = bcut(16 * F)
        w1s, w2s, w1t, w12, b1b = bcut(64), bcut(F), bcut(F), bcut(F), bcut(P)
        b1c, pcol, dnext = bcut(1), bcut(1), bcut(1, i32)
        rowno, partno = bcut(P, i32), bcut(1, i32)
        ncut = cutter(big[:, 0:18 * EC]) if 18 * EC >= QW * CW * TW + 2 * ES else bcut
        ndeg, nrow, n1, n2, n3 = [bcut(NCOL) for _ in range(5)]
        ni = bcut(NCOL, i32)
        ntot, nexc = bcut(NCH), bcut(NCH)
        aggb = [[c(CW * TW).rearrange("p (c w) -> p c w", w=TW) for _ in range(QW)] for c in (bcut, ncut)]
        xb = [rm(ncut(ES)) for _ in range(2)]

        psum = ctx.enter_context(nc.psum_tensor("psum", [P, 8 * 512], f32))
        bank = [psum[:, 512 * k:512 * (k + 1)] for k in range(8)]
        T0, U, T1 = [psum[:, 1024 * k:1024 * k + ES] for k in range(3)]
        CARRY = bank[6][:, 0:F]
        SETUP = bank[7]

        names = """filled loaded attr_loaded w_loaded bd_loaded zeroed before_added zrow_written
            iota_set matrices_set dst0_turned link_set count_carry roots_asked roots_set
            w1_turned w1t_set w12_made w12_set rows_set
            consumed idx_copied h_ready h_turned hT_copied src_turned same_set hot_ready hot_used y_ready y_used
            msg_ready sum_ready sums_copied oi_ready hist_done tot_ready offsets_made
            node_asked node_made
            scanned run_copied ends_ready carry_ready bound_ready bound_written
            side_in side_gathered side_idx side_taken side_made side_written
            pool_passed d_taken fin_taken fin_made fin_idx""".split()
        names += [f"{n}{b}" for n in ("gathered", "run_written", "agg_loaded", "node_written", "fin_loaded",
                                      "scattered") for b in range(2)]
        names += [f"{n}_{st}" for n in ("ln_asked", "ln_done") for st in ("l0", "q1", "q3", "q4", "n", "d")]
        names += [f"{n}_{st}" for n in ("v_ready", "v_turned", "v_copied", "u_ready") for st in ("q2", "q4", "n", "d")]
        S = {n: sem(n) for n in names}
        added = [sem(f"added{k}") for k in range(QW)]
        SIDE_WRITTEN = 16 * (NFULL + (NPF > 0) + (NTAIL > 0)) + 1
        V, A, T = nc.vector, nc.scalar, nc.tensor

        def flat(t):
            return t.rearrange("p c e -> p (c e)")

        def edge_rows(table, c):
            t = table[0:EP, :].rearrange("(p c j) e -> p c (j e)", c=ECH, j=CW)
            return t[:, bass.ds(c, 1), :].rearrange("p a e -> p (a e)")

        def node_rows(table, c, n=NCH):
            t = table[0:n * CH, :].rearrange("(c p j) e -> p c (j e)", p=P, j=CW)
            return t[:, bass.ds(c, 1), :].rearrange("p a e -> p (a e)")

        def cols(t, c):
            s = bass.ds(c * CW, CW)
            return t[:, s] if len(t.shape) == 2 else t[:, s, :]

        def coef(t, k, c):
            return t[:, k, bass.ds(c * CW, CW)]

        def over_f(t):
            return t.unsqueeze(2).to_broadcast([P, CW, F])

        def over_c(t):
            return t.unsqueeze(1).to_broadcast([P, CW, F])

        def load_edges(q, tile, line, s, k=1):
            for a, z in ((0, EFULL // 16 * 16), (EFULL // 16 * 16, EFULL)):
                if z > a:
                    part = line[a * EC:z * EC] if k == 1 else line[a * EC:z * EC, :].rearrange("n k -> (n k)")
                    q.dma_start(tile[a:z, :], part.rearrange("(p c) -> p c", c=EC * k)).then_inc(s, 16)
            part = line[EFULL * EC:E] if k == 1 else line[EFULL * EC:E, :].rearrange("n k -> (n k)")
            q.dma_start(tile[EFULL:EFULL + 1, 0:ETAIL * k], part.rearrange("(a c) -> a c", a=1)).then_inc(s, 16)

        EDGE_DMAS = 1 + sum(z > a for a, z in ((0, EFULL // 16 * 16), (EFULL // 16 * 16, EFULL)))

        def step_of(q, i, b):
            return i * 2 + (q * ECH + b)

        def table_in(q):
            return {1: nodes, 2: run1, 3: run2, 4: run3}.get(q, run4a if q % 2 else run4b)

        def table_out(q):
            return {1: run1, 2: run2, 3: run3}.get(q, run4b if q % 2 else run4a)

        Q_N, Q_D = 5, 5 + SP_N
        Q_LAST = 3 + PASSES
        assert Q_D + 2 <= Q_LAST

        def layer3(eng, body, end):
            for q0, pairs, side in ((Q_N, SP_N // 2, "n"), (Q_D, 1, "d"), (Q_D + 2, (Q_LAST - Q_D - 2) // 2, None)):
                if pairs == 0:
                    continue
                with eng.Fori(0, pairs) as kk:
                    for h in range(2):
                        q = kk * 2 + (q0 + h)
                        with eng.Fori(0, EB) as i:
                            body(q0 + h, q, i, side, kk * (2 * EB) + (i + h * EB))
                        end(q0 + h, q)
            with eng.Fori(0, EB) as i:
                body(Q_LAST, Q_LAST, i, None, 0)
            end(Q_LAST, Q_LAST)
        assert (Q_LAST - Q_D - 2) % 2 == 0

        block = ctx.enter_context(nc.Block())

        @block.sync
        def _(sp):
            sp.wait_ge(S["filled"], 1)
            load_edges(sp, dsti[:, :], dst, S["loaded"])
            load_edges(sp, srci[:, :], src, S["loaded"])
            with nc.allow_non_contiguous_dma(reason="one value of each partition"):
                sp.dma_start(dnext[0:EFULL, :], dst[EC:EC + (EFULL - 1) * EC + 1:EC].rearrange("(p a) -> p a", a=1))\
                  .then_inc(S["loaded"], 16)
            load_edges(sp, attr_s, attr, S["attr_loaded"], 2)
            sp.dma_start(w1s[0:F, :], w1).then_inc(S["w_loaded"], 16)
            sp.dma_start(w2s[0:64, :], w2).then_inc(S["w_loaded"], 16)
            with nc.allow_non_contiguous_dma(reason="a bias down the partitions"):
                sp.dma_start(b1c[0:64, :], b1.rearrange("(p a) -> p a", a=1)).then_inc(S["w_loaded"], 16)
            sp.dma_start(b2r[:, :], b2.rearrange("(a f) -> a f", a=1).to_broadcast([P, F])).then_inc(S["w_loaded"], 16)
            sp.dma_start(blr[:, :], bl.rearrange("(a f) -> a f", a=1).to_broadcast([P, F])).then_inc(S["w_loaded"], 16)
            for t in range(QW):
                r = slice(F * t, F * t + F)
                sp.dma_start(w0r[r, :].rearrange("f (k o) -> f k o", o=F), w0.rearrange("a b f o -> f (a b) o"))\
                  .then_inc(S["w_loaded"], 16)
                sp.dma_start(bda[r, r], wl[0:F, :]).then_inc(S["w_loaded"], 16)
                sp.dma_start(bdb[r, r], wl[F:2 * F, :]).then_inc(S["w_loaded"], 16)
            for r in (run1, run2, run3, run4a, run4b):
                sp.dma_start(r[ZROW:ZROW + 1, :], zrow[:, :]).then_inc(S["zrow_written"], 16)
            with sp.Fori(1, NCH) as c:
                for k in range(QW):
                    sp.dma_start(node_rows(agg0[k], c), flat(ms[1])).then_inc(S["zeroed"], 16)
            sp.wait_ge(S["w12_set"], 1)
            for t in range(QW):
                r = slice(F * t, F * t + F)
                sp.dma_start(bd12[r, r], w12[0:F, :]).then_inc(S["bd_loaded"], 16)

            for k in range(QW):
                sp.wait_ge(added[k], 16 + 16 * (EC // QW))

            def node_body(i, last):
                for b in range(2):
                    sp.wait_ge(S["node_asked"], i * 2 + (b + 1))
                    for k in range(QW):
                        sp.dma_start(flat(aggb[b][k]), node_rows(agg0[k], i * 2 + b)).then_inc(S[f"agg_loaded{b}"], 16)
                    s = S[f"agg_loaded{b}"]
                    if not (last and b):
                        sp.dma_start(flat(xb[b]), node_rows(x, i * 2 + b, NFULL)).then_inc(s, 16)
                    else:
                        if NPF:
                            lo = NFULL * CH
                            sp.dma_start(flat(xb[b][0:NPF]), x[lo:lo + NPF * CW, :].rearrange("(p j) e -> p (j e)", j=CW))\
                              .then_inc(s, 16)
                        if NTAIL:
                            lo = NFULL * CH + NPF * CW
                            sp.dma_start(flat(xb[b][NPF:NPF + 1, 0:NTAIL]), x[lo:N, :].rearrange("(p j) e -> p (j e)", p=1))\
                              .then_inc(s, 16)
                for b in range(2):
                    sp.wait_ge(S["node_made"], i * 2 + (b + 1))
                    sp.dma_start(node_rows(nodes, i * 2 + b), flat(g36[b])).then_inc(S[f"node_written{b}"], 16)

            if NCH > 2:
                with sp.Fori(0, NCH // 2 - 1) as i:
                    node_body(i, False)
            node_body(NCH // 2 - 1, True)

            def write_runs(q0, q, i):
                for b in range(2):
                    sp.wait_ge(S["run_copied"], q * ECH + (i * 2 + (b + 3 - ECH)))
                    sp.dma_start(edge_rows(table_out(q0), i * 2 + b), flat(ro[b])).then_inc(S[f"run_written{b}"], 16)

            def write_bound(q0, q):
                sp.wait_ge(S["bound_ready"], q)
                sp.dma_start(table_out(q0)[EP:EP + P, :], bound[:, :]).then_inc(S["bound_written"], 16)

            for q in range(1, 5):
                with sp.Fori(0, EB) as i:
                    write_runs(q, q, i)
                write_bound(q, q)

            def side_in(n):
                sp.wait_ge(S["side_taken"], n + 1)
                sp.dma_start(flat(sx), node_rows(nodes, n)).then_inc(S["side_in"], 16)

            def side_out(n):
                sp.wait_ge(S["side_made"], n + 1)
                sp.dma_start(node_rows(out, n, NFULL), flat(su)).then_inc(S["side_written"], 16)

            def side_out_last():
                sp.wait_ge(S["side_made"], NCH)
                lo = NFULL * CH
                if NPF:
                    sp.dma_start(out[lo:lo + NPF * CW, :].rearrange("(p j) e -> p (j e)", j=CW), flat(su[0:NPF]))\
                      .then_inc(S["side_written"], 16)
                if NTAIL:
                    lo += NPF * CW
                    sp.dma_start(out[lo:N, :].rearrange("(p j) e -> p (j e)", p=1), flat(su[NPF:NPF + 1, 0:NTAIL]))\
                      .then_inc(S["side_written"], 16)

            for q in range(Q_N, Q_D):
                last = q == Q_D - 1
                n0 = (q - Q_N) * EB
                if not last or EB > 1:
                    with sp.Fori(0, EB - last) as i:
                        side_in(i + n0)
                        side_out(i + n0)
                        write_runs(q, q, i)
                if last:
                    side_in(NCH - 1)
                    side_out_last()
                    write_runs(q, q, EB - 1)
                write_bound(q, q)
            for q in range(Q_D, Q_D + 2):
                with sp.Fori(0, EB) as i:
                    n = i + (q - Q_D) * EB
                    sp.wait_ge(S["d_taken"], n + 1)
                    for k, table in enumerate((run1, run2, run3)):
                        sp.dma_start(flat(sr[k]), edge_rows(table, n)).then_inc(S["side_in"], 16)
                    write_runs(q, q, i)
                write_bound(q, q)
            for q in range(Q_D + 2, Q_LAST + 1):
                with sp.Fori(0, EB) as i:
                    write_runs(q, q, i)
                write_bound(q, q)
            for b in range(2):
                sp.wait_ge(S[f"run_written{b}"], 16 * EB * Q_LAST + 1)
            sp.wait_ge(S["d_taken"], ECH + 1)
            with sp.Fori(0, EB) as i:
                for b in range(2):
                    sp.wait_ge(S["fin_taken"], i * 2 + (b + 1))
                    sp.dma_start(flat(sr[b]), edge_rows(table_out(Q_LAST), i * 2 + b)).then_inc(S[f"fin_loaded{b}"], 16)
            sp.wait_ge(S["bound_written"], 16 * Q_LAST)
            for b in range(2):
                sp.wait_ge(S[f"scattered{b}"], GI * EB)

        @block.gpsimd
        def _(pool):
            def wait(s, value):
                pool.wait_ge(s, value)
                pool.sem_inc(S["pool_passed"], 1)

            nc.gpsimd.iota(rowno, pattern=[[1, P]], base=0, channel_multiplier=0).then_inc(S["iota_set"], 1)
            nc.gpsimd.iota(ni[:, :], pattern=[[1, NCOL]], base=0, channel_multiplier=0).then_inc(S["iota_set"], 1)
            nc.gpsimd.iota(partno, pattern=[[0, 1]], base=0, channel_multiplier=1).then_inc(S["iota_set"], 1)
            nc.gpsimd.memset(ident[:, :], 0.0).then_inc(S["iota_set"], 1)
            wait(S["iota_set"], 4)
            nc.gpsimd.affine_select(out=ident[:, :], in_=ident[:, :], compare_op=ALU.not_equal, fill=1.0, base=0,
                                    pattern=[[-1, P]], channel_multiplier=1).then_inc(S["iota_set"], 1)

            def gather(table, w, index, q, i, b):
                g = step_of(q, i, b)
                wait(S["consumed"], g + 1)
                nc.gpsimd.tensor_copy(ii[b][:, :], cols(index, i * 2 + b)).then_inc(S["idx_copied"], 1)
                wait(S["idx_copied"], g + 1)
                for j in range(CW):
                    o = g36[b][:, j, :] if w == NW else gbuf[b][:, j, :]
                    pool.indirect_dma_start(o, None, table, bass.IndirectOffsetOnAxis(ii[b][:, j:j + 1], 0))\
                        .then_inc(S[f"gathered{b}"], 16)

            def scatter0(i, b):
                wait(S["oi_ready"], i * 2 + (b + 1))
                for n in range(NQ):
                    wait(S["sums_copied"], i * 2 * NQ + (b * NQ + n + 2))
                    for t in range(QW):
                        wait(added[t], i * (32 * NQ) + (16 + 16 * (b * NQ + n)))
                        j = n * QW + t
                        pool.indirect_dma_start(agg0[t], bass.IndirectOffsetOnAxis(oi[b][:, j:j + 1], 0), ms[b][:, j, :],
                                                None, compute_op=ALU.add).then_inc(added[t], 16)
                    if n == 0:
                        pool.sem_inc(S["before_added"], 1)

            wait(S["filled"], 1)
            for k in range(QW):
                pool.dma_start(node_rows(agg0[k], 0), flat(ms[1])).then_inc(added[k], 16)
            wait(S["rows_set"], 1)
            gather(x, F, rowi, 0, 0, 0)
            wait(S["zeroed"], 16 * QW * (NCH - 1))
            if EB > 1:
                with pool.Fori(0, EB - 1) as i:
                    gather(x, F, rowi, 0, i, 1)
                    scatter0(i, 0)
                    gather(x, F, rowi, 0, i + 1, 0)
                    scatter0(i, 1)
            gather(x, F, rowi, 0, EB - 1, 1)
            scatter0(EB - 1, 0)
            scatter0(EB - 1, 1)

            for b in range(2):
                wait(S[f"node_written{b}"], 16 * (NCH // 2) + 1)
            with pool.Fori(0, EB) as i:
                for b in range(2):
                    gather(nodes, NW, srci, 1, i, b)

            def table_whole(q):
                for b in range(2):
                    wait(S[f"run_written{b}"], (q - 1) * (16 * EB) + 1)
                wait(S["bound_written"], (q - 1) * 16)

            wait(S["zrow_written"], 16 * 5)
            for q in range(2, 5):
                table_whole(q)
                with pool.Fori(0, EB) as i:
                    for b in range(2):
                        gather(table_in(q), F, rowi, q, i, b)

            def body(q0, q, i, side, n):
                if side == "d":
                    wait(S["side_taken"], NCH + 1)
                    wait(S["d_taken"], n + 1)
                    nc.gpsimd.tensor_copy(di[:, :], cols(dsti, n)).then_inc(S["side_idx"], 1)
                    wait(S["side_idx"], n + 1)
                    for j in range(CW):
                        pool.indirect_dma_start(sx[:, j, :], None, nodes, bass.IndirectOffsetOnAxis(di[:, j:j + 1], 0))\
                            .then_inc(S["side_gathered"], 16)
                for b in range(2):
                    gather(table_in(q0), F, rowi, q, i, b)

            def end(q0, q):
                if q0 != Q_LAST:
                    table_whole(q + 1)

            table_whole(Q_N)
            layer3(pool, body, end)

            wait(S["side_written"], SIDE_WRITTEN)
            with pool.Fori(0, EB) as i:
                for b in range(2):
                    wait(S["fin_made"], i * 2 + (b + 1))
                    nc.gpsimd.tensor_copy(ii[b][:, :], cols(outi, i * 2 + b)).then_inc(S["fin_idx"], 1)
                    wait(S["fin_idx"], i * 2 + (b + 1))
                    for j in range(CW):
                        pool.indirect_dma_start(out, bass.IndirectOffsetOnAxis(ii[b][:, j:j + 1], 0), ro[b][:, j, :], None,
                                                bounds_check=N - 1, oob_is_err=False).then_inc(S[f"scattered{b}"], 16)

        @block.vector
        def _(dve):
            def dr():
                nc.vector.drain()

            def floordiv(xv, d, qv, r, t, ti):
                V.tensor_scalar(ti, xv, 1.0 / d, None, ALU.mult)
                dr()
                V.tensor_copy(qv, ti)
                dr()
                V.scalar_tensor_tensor(r, qv, -float(d), xv, ALU.mult, ALU.add)
                dr()
                V.tensor_scalar(t, r, 0.0, None, ALU.is_lt)
                dr()
                V.tensor_tensor(qv, qv, t, ALU.subtract)
                V.scalar_tensor_tensor(r, t, float(d), r, ALU.mult, ALU.add)
                dr()
                V.tensor_scalar(t, r, float(d), None, ALU.is_ge)
                dr()
                V.tensor_tensor(qv, qv, t, ALU.add)
                V.scalar_tensor_tensor(r, t, -float(d), r, ALU.mult, ALU.add)
                dr()

            dve.sem_inc(S["consumed"], 2)
            for s in ("before_added", "run_written0", "run_written1", "node_written0", "node_written1", "sum_ready", "hT_copied", "same_set", "sums_copied",
                      "side_taken", "d_taken", "side_written"):
                dve.sem_inc(S[s], 1)
            for s in ("y_used", "hot_used", "run_copied", "fin_taken", "node_asked"):
                dve.sem_inc(S[s], 2)
            V.memset(srci[:, :], SRC_PAD)
            V.memset(dsti[:, :], DST_PAD)
            V.memset(dnext, -1)
            V.memset(attr_s, 0.0)
            V.memset(flat(ms[1]), 0.0)
            V.memset(zrow[:, :], 0.0)
            V.memset(epsc[:, :], EPS)
            for t in (bd12, bda, bdb):
                V.memset(t[:, :], 0.0)
            dr()
            V.memset(nil, 0.0).then_inc(S["filled"], 1)
            V.memset(ones, 1.0)
            V.memset(e3, 1.0)
            V.memset(msg[:, :, F:TW], 1.0)
            V.memset(cuts, 1.0)
            dr()
            V.memset(cuts.rearrange("p (c j) -> p c j", j=CW)[:, :, 0:1], 0.0)
            dve.wait_ge(S["iota_set"], 5)
            V.tensor_copy(iotar, rowno)
            V.tensor_copy(iotaw, ni)
            V.tensor_copy(pcol, partno)
            dr()
            V.tensor_copy(iotan, iotaw)
            V.tensor_scalar(after, iotar, pcol, None, ALU.is_gt)
            V.tensor_scalar(before, iotar, pcol, None, ALU.is_lt)
            dve.wait_ge(S["loaded"], 16 * (2 * EDGE_DMAS + 1))
            V.tensor_copy(dstf, dsti[:, :])
            V.tensor_copy(srcf, srci[:, :])
            dr()
            V.tensor_scalar(e1, dstf, float(N - 1), None, ALU.min)
            dr()
            V.tensor_copy(rowi[:, :], e1).then_inc(S["rows_set"], 1)
            V.tensor_scalar(pad_to, pcol.to_broadcast([P, CW]), float(N), None, ALU.add)
            V.memset(keep[:, 0:1], 0.0)
            V.tensor_tensor(keep[:, 1:EC], dstf[:, 1:EC], dstf[:, 0:EC - 1], ALU.is_equal)
            V.tensor_copy(e2[:, 0:1], dnext)
            dr()
            V.tensor_tensor(keep[:, EC:EC + 1], dstf[:, EC - 1:EC], e2[:, 0:1], ALU.is_equal)
            V.tensor_scalar(start[:, :], dstf, dstf[:, 0:1], None, ALU.is_equal).then_inc(S["matrices_set"], 1)
            dr()
            V.scalar_tensor_tensor(e1, keep[:, 1:EC + 1], float(1 << 20), dstf, ALU.mult, ALU.add)
            kv = keep[:, 0:EC].rearrange("p (c j) -> p c j", j=CW)
            for f in range(F):
                V.tensor_copy(keepx[:, :, :].rearrange("p c (f j) -> p c f j", j=CW)[:, :, f, :], kv)
            dr()
            V.memset(keepx[:, :, :].rearrange("p c (f j) -> p (c f) j", j=CW)[:, :, 0:1], 0)
            V.tensor_copy(outi[:, :], e1)
            V.tensor_tensor_scan(e2, keep[:, 0:EC], e3, 0.0, ALU.mult, ALU.add)
            dve.wait_ge(S["dst0_turned"], 1)
            V.scalar_tensor_tensor(link[:, :], SETUP[:, 0:P], dstf[:, EC - 1:EC], after, ALU.is_equal, ALU.mult)\
                .then_inc(S["link_set"], 1)
            dve.wait_ge(S["count_carry"], 1)
            dr()
            V.tensor_copy(e1[:, 0:1], SETUP[:, 0:1])
            dr()
            V.scalar_tensor_tensor(e3, start[:, :], e1[:, 0:1], e2, ALU.mult, ALU.add)
            dr()
            V.tensor_scalar(e1, e3, 1.0, None, ALU.add)
            V.tensor_scalar(e2, e3, 1.0, None, ALU.max)
            dr()
            V.reciprocal(coefD[:, 0, :], e1)
            V.reciprocal(coefD[:, 1, :], e2).then_inc(S["roots_asked"], 1)
            dve.wait_ge(S["roots_set"], 2)
            V.reciprocal(coefD[:, 2, :], e1)
            V.reciprocal(coefD[:, 3, :], e2)
            floordiv(dstf, CH, e1, e2, e3, ei)
            floordiv(e2, CW, wpart, wfree, e3, ei)
            V.scalar_tensor_tensor(wfree, e1, float(CW), wfree, ALU.mult, ALU.add)
            dve.wait_ge(S["attr_loaded"], 16 * EDGE_DMAS)
            av = attr_s.rearrange("p (c k) -> p c k", k=2)
            for m in range(4):
                cm = float(-1.0 + m * (2.0 / 3.0))
                dr()
                V.tensor_scalar(e1, av[:, :, 0], -cm, None, ALU.add)
                dr()
                V.scalar_tensor_tensor(e1, e1, -1.0, e1, ALU.mult, ALU.max)
                dr()
                V.tensor_scalar(e1, e1, -1.5, 1.0, ALU.mult, ALU.add)
                dr()
                V.tensor_scalar(e1, e1, 0.0, None, ALU.max)
                for k in range(4):
                    ck = float(-1.0 + k * (2.0 / 3.0))
                    V.tensor_scalar(e2, av[:, :, 1], -ck, None, ALU.add)
                    dr()
                    V.scalar_tensor_tensor(e2, e2, -1.0, e2, ALU.mult, ALU.max)
                    dr()
                    V.tensor_scalar(e2, e2, -1.5, 1.0, ALU.mult, ALU.add)
                    dr()
                    V.scalar_tensor_tensor(basis[:, :, 4 * m + k], e2, 0.0, e1, ALU.max, ALU.mult)
                    dr()
            dve.wait_ge(S["w_loaded"], 16 * (5 + 3 * QW))
            V.tensor_copy(b1b[0:64, :], b1c[0:64, :].to_broadcast([64, P])).then_inc(S["w1t_set"], 1)
            dve.wait_ge(S["w1_turned"], 1)
            V.tensor_copy(w1t[0:64, :], SETUP[0:64, 0:F]).then_inc(S["w1t_set"], 1)
            dve.wait_ge(S["w12_made"], 1)
            V.tensor_copy(w12[0:F, :], SETUP[0:F, 64:64 + F]).then_inc(S["w12_set"], 1)
            V.tensor_copy(b12[:, :], SETUP[:, 128:128 + F])
            dr()
            V.tensor_tensor(b12n[:, :], b12[:, :], b2r[:, :], ALU.add)
            dr()

            def layernorm(st, n, xin, h, signal=None):
                V.tensor_reduce(small[:, 0, :], xin, AX.X, ALU.add)
                dr()
                V.tensor_scalar(small[:, 1, :], small[:, 0, :], -1.0 / F, None, ALU.mult)
                dr()
                ins = V.tensor_tensor(tb, xin, over_f(small[:, 1, :]), ALU.add)
                ins.then_inc(S[f"ln_asked_{st}"], 1)
                dve.wait_ge(S[f"ln_done_{st}"], n * 2 + 1)
                if signal:
                    dve.sem_inc(S[signal], 1)
                V.tensor_reduce(small[:, 2, :], tc, AX.X, ALU.add).then_inc(S[f"ln_asked_{st}"], 1)
                dve.wait_ge(S[f"ln_done_{st}"], n * 2 + 2)
                V.reciprocal(small[:, 4, :], small[:, 3, :])
                dr()
                return V.scalar_tensor_tensor(h, tb, 0.0, over_f(small[:, 4, :]), ALU.max, ALU.mult)

            def chunk_arrived(q, i, b):
                dve.wait_ge(S[f"gathered{b}"], (q * EB + i) * GI + GI)

            def layer0_chunk(i, b):
                chunk_arrived(0, i, b)
                g = i * 2 + b
                layernorm("l0", g, gbuf[b], ta, "consumed")
                dr()
                V.tensor_copy(srcc[b], cols(srcf, g))
                dr()
                dve.sem_inc(S["h_ready"], 1)
                for n in range(NQ):
                    k = i * (2 * NQ) + (b * NQ + n)
                    qc = bass.ds(i * (2 * CW) + (b * CW + n * QW), QW)
                    dve.wait_ge(S["sum_ready"], k + 1)
                    dve.wait_ge(S["src_turned"], k + 1)
                    V.tensor_tensor(s4, bank[4].rearrange("p (t q) -> p t q", t=QW),
                                    srcf[:, qc].unsqueeze(2).to_broadcast([P, QW, P]), ALU.is_equal)\
                        .then_inc(S["same_set"], 1)
                    dr()
                    V.tensor_tensor(s4m, s4, before.unsqueeze(1).to_broadcast([P, QW, P]), ALU.mult)
                    dve.wait_ge(S["hot_used"], 4 * k + 2)
                    V.tensor_tensor(hotp, iotar.unsqueeze(1).to_broadcast([P, QW, P]),
                                    wpart[:, qc].unsqueeze(2).to_broadcast([P, QW, P]), ALU.is_equal)
                    dr()
                    V.tensor_reduce(dup[:, n * QW:(n + 1) * QW], s4m, AX.X, ALU.add)
                    for t in range(QW):
                        col = i * (2 * CW) + (b * CW + n * QW + t)
                        dve.wait_ge(S["hot_used"], 4 * k + (t + 1))
                        V.tensor_scalar(hot[t % 2], iotan, wfree[:, bass.ds(col, 1)], None, ALU.is_equal)\
                            .then_inc(S["hot_ready"], 1)
                        dve.wait_ge(S["y_ready"], 4 * k + (t + 1))
                        V.tensor_tensor(ym, bank[2 + t % 2].rearrange("p (k o) -> p k o", k=16),
                                        basis[:, bass.ds(col, 1), :].rearrange("p a k -> p (a k)").unsqueeze(2).to_broadcast([P, 16, F]),
                                        ALU.mult).then_inc(S["y_used"], 1)
                        dr()
                        V.tensor_reduce(msg[:, t, 0:F], ym.rearrange("p k o -> p o k"), AX.X, ALU.add)
                        dr()
                    dve.sem_inc(S["msg_ready"], 1)
                V.tensor_scalar(dup, dup, 1.0, None, ALU.min)
                V.tensor_tensor(small[:, 5, :], pad_to, cols(srcf, g), ALU.subtract)
                dr()
                V.tensor_tensor(small[:, 5, :], small[:, 5, :], dup, ALU.mult)
                dr()
                dve.wait_ge(S["before_added"], i * 2 + (b + 1))
                V.tensor_tensor(oi[b], small[:, 5, :], cols(srcf, g), ALU.add).then_inc(S["oi_ready"], 1)

            with dve.Fori(0, EB) as i:
                for b in range(2):
                    layer0_chunk(i, b)

            dve.wait_ge(S["hist_done"], 1)
            V.tensor_copy(ndeg[:, 0:HW], bank[0][:, 0:HW])
            V.tensor_copy(ndeg[:, HW:NCOL], bank[1][:, 0:HW])
            dr()
            V.tensor_tensor_scan(n1, cuts, ndeg, 0.0, ALU.mult, ALU.add)
            dr()
            n1v = n1.rearrange("p (c j) -> p c j", j=CW)
            V.tensor_copy(ntot, n1v[:, :, CW - 1]).then_inc(S["tot_ready"], 1)
            dve.wait_ge(S["offsets_made"], 1)
            V.tensor_copy(n3[:, 0:NCH], SETUP[:, NCH:2 * NCH])
            dr()
            V.tensor_tensor_scan(nexc, ones[:, 0:NCH], n3[:, 0:NCH], 0.0, ALU.mult, ALU.add)
            dr()
            V.tensor_tensor(nexc, nexc, n3[:, 0:NCH], ALU.subtract)
            dr()
            V.tensor_tensor(nexc, nexc, SETUP[:, 0:NCH], ALU.add)
            dr()
            V.tensor_tensor(n1v, n1v, nexc.unsqueeze(2).to_broadcast([P, NCH, CW]), ALU.add)
            dr()
            V.tensor_scalar(n1, n1, -1.0, None, ALU.add)
            dr()
            floordiv(n1, EC, n2, n3, nrow, ni)
            V.tensor_tensor(nrow, n3, ndeg, ALU.is_lt)
            V.tensor_scalar(n2, n2, float(EP), None, ALU.add)
            dr()
            V.tensor_tensor(n2, n2, n1, ALU.subtract)
            dr()
            V.tensor_tensor(n2, n2, nrow, ALU.mult)
            dr()
            V.tensor_tensor(nrow, n2, n1, ALU.add)
            V.tensor_scalar(n3, ndeg, 1.0, None, ALU.min)
            dr()
            V.tensor_scalar(nrow, nrow, -float(ZROW), None, ALU.add)
            dr()
            V.tensor_tensor(nrow, nrow, n3, ALU.mult)
            dr()
            V.tensor_scalar(nrow, nrow, float(ZROW), None, ALU.add)
            for b in range(2):
                V.memset(g36[b][:, :, F + 3:NW], 0.0)
            dr()

            def node_chunk(i, b, loads):
                dve.wait_ge(S[f"agg_loaded{b}"], loads)
                dve.wait_ge(S[f"node_written{b}"], i * 16 + 1)
                a = aggb[b]
                V.tensor_tensor(a[0], a[0], a[1], ALU.add)
                V.tensor_tensor(a[2], a[2], a[3], ALU.add)
                dr()
                V.tensor_tensor(a[0], a[0], a[2], ALU.add)
                dr()
                V.tensor_tensor(g36[b][:, :, 0:F], a[0][:, :, 0:F], xb[b], ALU.add)
                V.tensor_copy(g36[b][:, :, F], a[0][:, :, F])
                V.tensor_copy(g36[b][:, :, F + 1], cols(ndeg, i * 2 + b))
                V.tensor_copy(g36[b][:, :, F + 2], cols(nrow, i * 2 + b))
                dr()
                dve.sem_inc(S["node_asked"], 1)
                dve.sem_inc(S["node_made"], 1)

            PER = 16 * (QW + 1)
            if NCH > 2:
                with dve.Fori(0, NCH // 2 - 1) as i:
                    for b in range(2):
                        node_chunk(i, b, i * PER + PER)
            node_chunk(NCH // 2 - 1, 0, NCH // 2 * PER)
            node_chunk(NCH // 2 - 1, 1, NCH // 2 * PER - 16 + 16 * ((NPF > 0) + (NTAIL > 0)))

            tbf = flat(tb).rearrange("p (f j) -> p f j", j=CW)
            U3 = rm(U)
            for t in rff:
                V.memset(t, 0.0)
            V.memset(firstrun[:, :], 0.0)
            dve.wait_ge(S["bd_loaded"], 16 * QW)

            def scan_chunk(q, i, b):
                c = i * 2 + b
                g1 = q * ECH + (i * 2 + (b + 1 - ECH))
                V.tensor_tensor(tbf, mf, cols(start, c).unsqueeze(1).to_broadcast([P, F, CW]), ALU.mult)
                dr()
                V.tensor_reduce(frpart[:, :], tbf, AX.X, ALU.add)
                V.scalar_tensor_tensor(mf[:, :, 0], rf[1 - b][:, :, CW - 1], keep[:, bass.ds(c * CW, 1)], mf[:, :, 0],
                                       ALU.mult, ALU.add)
                dr()
                V.tensor_tensor(firstrun[:, :], firstrun[:, :], frpart[:, :], ALU.add)
                dve.wait_ge(S["run_copied"], g1)
                V.tensor_tensor_scan(rff[b], keepx[:, bass.ds(c, 1), :].rearrange("p a e -> p (a e)"), mff, 0.0,
                                     ALU.mult, ALU.add).then_inc(S["scanned"], 1)
                dr()

            def pass_end(q0, q):
                if q0 > 1:
                    dve.wait_ge(S["bound_written"], q * 16 - 16)
                V.tensor_copy(ends[:, :], rf[1][:, :, CW - 1]).then_inc(S["ends_ready"], 1)
                dve.wait_ge(S["carry_ready"], q)
                V.tensor_copy(carries[:, min(q0 - 1, 3), :], CARRY)
                V.tensor_tensor(bound[:, :], firstrun[:, :], CARRY, ALU.add)
                dr()
                V.memset(firstrun[:, :], 0.0)
                dr()
                dve.sem_inc(S["bound_ready"], 1)

            def pass1(i, b):
                c = i * 2 + b
                chunk_arrived(1, i, b)
                g = g36[b]
                sl = bass.ds(c * CW, CW)
                V.tensor_copy(cols(rowi, c), g[:, :, F + 2])
                V.tensor_copy(cols(xs, c), g[:, :, 0:F])
                V.tensor_scalar(small[:, 0, :], g[:, :, F + 1], 1.0, None, ALU.add)
                V.tensor_scalar(small[:, 1, :], g[:, :, F + 1], 1.0, None, ALU.max)
                V.tensor_scalar(small[:, 2, :], g[:, :, F], 1.0, None, ALU.max)
                dr()
                dve.sem_inc(S["consumed"], 1)
                V.reciprocal(coefS[:, 0:2, sl], small[:, 0:2, :]).then_inc(S["roots_asked"], 1)
                dve.wait_ge(S["roots_set"], i * 2 + (b + 3))
                V.reciprocal(coefS[:, 2:5, sl], small[:, 0:3, :])
                dr()
                layernorm("q1", c, cols(xs, c), cols(hs, c))
                dr()
                V.tensor_tensor(mfr, cols(hs, c), over_f(coef(coefS, 2, c)), ALU.mult)
                dr()
                scan_chunk(1, i, b)

            with dve.Fori(0, EB) as i:
                for b in range(2):
                    pass1(i, b)
            pass_end(1, 1)

            def pass2(i, b):
                c = i * 2 + b
                chunk_arrived(2, i, b)
                V.tensor_tensor(ta, gbuf[b], over_f(coef(coefS, 2, c)), ALU.mult).then_inc(S["consumed"], 1)
                V.tensor_tensor(tb, cols(hs, c), over_f(coef(coefS, 0, c)), ALU.mult)
                dr()
                V.tensor_tensor(ta, ta, tb, ALU.add).then_inc(S["v_ready_q2"], 1)
                dve.wait_ge(S["u_ready_q2"], c + 1)
                V.tensor_tensor(cols(hs, c), U3, over_c(b12[:, :]), ALU.add)
                dr()
                V.tensor_tensor(mfr, cols(hs, c), over_f(coef(coefS, 2, c)), ALU.mult)
                dr()
                scan_chunk(2, i, b)

            with dve.Fori(0, EB) as i:
                for b in range(2):
                    pass2(i, b)
            pass_end(2, 2)

            def pass3(i, b):
                c = i * 2 + b
                chunk_arrived(3, i, b)
                V.tensor_tensor(ta, gbuf[b], over_f(coef(coefS, 2, c)), ALU.mult).then_inc(S["consumed"], 1)
                V.tensor_tensor(tb, cols(hs, c), over_f(coef(coefS, 0, c)), ALU.mult)
                dr()
                V.tensor_tensor(ta, ta, tb, ALU.add)
                dr()
                V.tensor_tensor(ta, ta, over_c(b2r[:, :]), ALU.add)
                dr()
                V.scalar_tensor_tensor(cols(xs, c), ta, 0.0, cols(xs, c), ALU.max, ALU.add)
                dr()
                layernorm("q3", c, cols(xs, c), cols(hs, c))
                dr()
                V.tensor_copy(mfr, cols(hs, c))
                dr()
                scan_chunk(3, i, b)

            with dve.Fori(0, EB) as i:
                for b in range(2):
                    pass3(i, b)
            pass_end(3, 3)

            def pass4(i, b):
                c = i * 2 + b
                chunk_arrived(4, i, b)
                V.tensor_tensor(ta, gbuf[b], over_f(coef(coefS, 1, c)), ALU.mult).then_inc(S["consumed"], 1)
                V.tensor_copy(su, cols(hs, c))
                dr()
                dve.sem_inc(S["v_ready_q4"], 1)
                dve.wait_ge(S["u_ready_q4"], c + 1)
                V.tensor_tensor(tb, U3, over_c(blr[:, :]), ALU.add)
                V.scalar_tensor_tensor(coef(coefS, 0, c), coef(coefS, 4, c), 1.0 - ALPHA, coef(coefS, 3, c), ALU.mult, ALU.mult)
                dr()
                V.scalar_tensor_tensor(cols(xs, c), tb, 0.0, cols(xs, c), ALU.max, ALU.add)
                dr()
                layernorm("q4", c, cols(xs, c), ta)
                dr()
                V.tensor_tensor(mfr, ta, over_f(coef(coefS, 4, c)), ALU.mult)
                dr()
                V.tensor_scalar(cols(hs, c), mfr, ALPHA, None, ALU.mult)
                scan_chunk(4, i, b)

            with dve.Fori(0, EB) as i:
                for b in range(2):
                    pass4(i, b)
            pass_end(4, 4)

            sxx = sx[:, :, 0:F]

            def side_nodes(n):
                dve.wait_ge(S["side_in"], n * 16 + 16)
                dve.wait_ge(S["side_written"], n * 16 + 1)
                layernorm("n", n * 3, sxx, su).then_inc(S["v_ready_n"], 1)
                dve.wait_ge(S["u_ready_n"], n * 2 + 1)
                V.tensor_tensor(ta, U3, over_c(b12n[:, :]), ALU.add)
                dr()
                V.scalar_tensor_tensor(sxx, ta, 0.0, sxx, ALU.max, ALU.add)
                dr()
                layernorm("n", n * 3 + 1, sxx, su).then_inc(S["v_ready_n"], 1)
                dve.wait_ge(S["u_ready_n"], n * 2 + 2)
                V.tensor_tensor(ta, U3, over_c(blr[:, :]), ALU.add)
                dr()
                V.scalar_tensor_tensor(sxx, ta, 0.0, sxx, ALU.max, ALU.add)
                dr()
                layernorm("n", n * 3 + 2, sxx, ta)
                dr()
                V.scalar_tensor_tensor(su, ta, ALPHA, sxx, ALU.mult, ALU.add).then_inc(S["side_made"], 1)
                dr()
                dve.sem_inc(S["side_taken"], 1)

            def side_dst(n):
                dve.wait_ge(S["side_in"], n * 48 + (16 * NCH + 48))
                dve.wait_ge(S["side_gathered"], n * GI + GI)
                dve.wait_ge(S["side_written"], SIDE_WRITTEN)

                def summed(k):
                    V.tensor_tensor(ta, over_f(cols(start, n)), over_c(carries[:, k, :]), ALU.mult)
                    dr()
                    V.tensor_tensor(ta, ta, sr[k], ALU.add)
                    dr()

                layernorm("d", n * 3, sxx, su)
                summed(0)
                V.tensor_tensor(ta, ta, over_f(coef(coefD, 2, n)), ALU.mult)
                V.tensor_tensor(tb, su, over_f(coef(coefD, 0, n)), ALU.mult)
                dr()
                V.tensor_tensor(ta, ta, tb, ALU.add).then_inc(S["v_ready_d"], 1)
                dve.wait_ge(S["u_ready_d"], n * 2 + 1)
                V.tensor_tensor(su, U3, over_c(b12[:, :]), ALU.add)
                summed(1)
                V.tensor_tensor(ta, ta, over_f(coef(coefD, 2, n)), ALU.mult)
                V.tensor_tensor(tb, su, over_f(coef(coefD, 0, n)), ALU.mult)
                dr()
                V.tensor_tensor(ta, ta, tb, ALU.add)
                dr()
                V.tensor_tensor(ta, ta, over_c(b2r[:, :]), ALU.add)
                dr()
                V.scalar_tensor_tensor(sxx, ta, 0.0, sxx, ALU.max, ALU.add)
                dr()
                layernorm("d", n * 3 + 1, sxx, su)
                summed(2)
                V.tensor_tensor(ta, ta, over_f(coef(coefD, 1, n)), ALU.mult).then_inc(S["v_ready_d"], 1)
                dve.wait_ge(S["u_ready_d"], n * 2 + 2)
                V.tensor_tensor(tb, U3, over_c(blr[:, :]), ALU.add)
                dr()
                V.scalar_tensor_tensor(sxx, tb, 0.0, sxx, ALU.max, ALU.add)
                dr()
                layernorm("d", n * 3 + 2, sxx, ta)
                dr()
                V.scalar_tensor_tensor(cols(xd, n), ta, ALPHA, sxx, ALU.mult, ALU.add)
                dr()
                dve.sem_inc(S["d_taken"], 1)

            def body(q0, q, i, side, n):
                if side == "n":
                    side_nodes(n)
                if side == "d":
                    side_dst(n)
                for b in range(2):
                    c = i * 2 + b
                    chunk_arrived(q, i, b)
                    V.tensor_tensor(mfr, gbuf[b], over_f(coef(coefS, 0, c)), ALU.mult).then_inc(S["consumed"], 1)
                    dr()
                    V.tensor_tensor(mfr, mfr, cols(hs, c), ALU.add)
                    dr()
                    scan_chunk(q, i, b)

            layer3(dve, body, pass_end)

            for b in range(2):
                dve.wait_ge(S[f"run_written{b}"], 16 * EB * Q_LAST + 1)

            def final(i, b, first=False):
                c = i * 2 + b
                dve.wait_ge(S[f"fin_loaded{b}"], i * 16 + 16)
                V.tensor_tensor(ta, over_f(cols(start, c)), over_c(carries[:, 3, :]), ALU.mult)
                dr()
                V.tensor_tensor(ta, ta, sr[b], ALU.add).then_inc(S["fin_taken"], 1)
                dr()
                V.tensor_tensor(ta, ta, over_f(coef(coefD, 3, c)), ALU.mult)
                dr()
                if not first:
                    dve.wait_ge(S[f"scattered{b}"], i * GI)
                V.scalar_tensor_tensor(ro[b], ta, 1.0 - ALPHA, cols(xd, c), ALU.mult, ALU.add)\
                    .then_inc(S["fin_made"], 1)
                dr()

            for b in range(2):
                final(0, b, True)
            if EB > 1:
                with dve.Fori(1, EB) as i:
                    for b in range(2):
                        final(i, b)

        @block.scalar
        def _(act):
            act.wait_ge(S["roots_asked"], 1)
            A.activation(e1, e1, ACT.Sqrt).then_inc(S["roots_set"], 1)
            A.activation(e2, e2, ACT.Sqrt).then_inc(S["roots_set"], 1)

            def layernorm(st, n):
                act.wait_ge(S[f"ln_asked_{st}"], n * 2 + 1)
                A.activation(tc, tb, ACT.Square).then_inc(S[f"ln_done_{st}"], 1)
                act.wait_ge(S[f"ln_asked_{st}"], n * 2 + 2)
                A.activation(small[:, 3, :], small[:, 2, :], ACT.Sqrt, bias=epsc[:, 0:1], scale=1.0 / F)\
                    .then_inc(S[f"ln_done_{st}"], 1)

            act.wait_ge(S["zeroed"], 16 * QW * (NCH - 1))
            for k in range(QW):
                act.wait_ge(added[k], 16)
            with act.Fori(0, EB) as i:
                for b in range(2):
                    layernorm("l0", i * 2 + b)
                    act.wait_ge(S["before_added"], i * 2 + (b + 1))

                    def turn_copy(n):
                        act.wait_ge(S["h_turned"], i * (2 * NQ) + (b * NQ + n + 1))
                        A.copy(hT[(b * NQ + n) % 2], bank[5][:, 0:P]).then_inc(S["hT_copied"], 1)

                    turn_copy(0)
                    for n in range(NQ):
                        if n + 1 < NQ:
                            turn_copy(n + 1)
                        act.wait_ge(S["sum_ready"], i * (2 * NQ) + (b * NQ + n + 2))
                        A.copy(ms[b][:, n * QW:(n + 1) * QW, :], bank[6][:, 0:QW * TW].rearrange("p (t w) -> p t w", w=TW))\
                            .then_inc(S["sums_copied"], 1)

            def run_copy(q, i, b):
                act.wait_ge(S["scanned"], q * ECH + (i * 2 + (b + 1 - ECH)))
                act.wait_ge(S[f"run_written{b}"], q * (16 * EB) + (i * 16 + (1 - 16 * EB)))
                A.copy(ro[b], rf[b].rearrange("p f j -> p j f")).then_inc(S["run_copied"], 1)

            def turned_copy(st, n, two=False):
                act.wait_ge(S[f"v_turned_{st}"], n + 1)
                if two:
                    A.copy(vT[1], T1)
                    act.drain()
                A.copy(vT[0], T0).then_inc(S[f"v_copied_{st}"], 1)

            with act.Fori(0, EB) as i:
                for b in range(2):
                    act.wait_ge(S["roots_asked"], i * 2 + (b + 2))
                    A.activation(small[:, 0:3, :], small[:, 0:3, :], ACT.Sqrt).then_inc(S["roots_set"], 1)
                    layernorm("q1", i * 2 + b)
                    run_copy(1, i, b)
            with act.Fori(0, EB) as i:
                for b in range(2):
                    turned_copy("q2", i * 2 + b)
                    run_copy(2, i, b)
            with act.Fori(0, EB) as i:
                for b in range(2):
                    layernorm("q3", i * 2 + b)
                    run_copy(3, i, b)
            with act.Fori(0, EB) as i:
                for b in range(2):
                    turned_copy("q4", i * 2 + b, True)
                    layernorm("q4", i * 2 + b)
                    run_copy(4, i, b)

            def body(q0, q, i, side, n):
                if side:
                    layernorm(side, n * 3)
                    turned_copy(side, n * 2)
                    layernorm(side, n * 3 + 1)
                    turned_copy(side, n * 2 + 1, side == "d")
                    layernorm(side, n * 3 + 2)
                for b in range(2):
                    run_copy(q, i, b)

            layer3(act, body, lambda q0, q: None)

        @block.tensor
        def _(pe):
            pe.wait_ge(S["iota_set"], 5)
            pe.wait_ge(S["matrices_set"], 1)
            T.transpose(SETUP[:, 0:P], dstf[:, 0:1].to_broadcast([P, P]), ident[:, :]).then_inc(S["dst0_turned"], 1)
            pe.wait_ge(S["link_set"], 1)
            T.matmul(SETUP[:, 0:1], link[:, :], e2[:, EC - 1:EC], start=True, stop=True).then_inc(S["count_carry"], 1)
            pe.wait_ge(S["w1t_set"], 1)
            T.transpose(SETUP[0:64, 0:F], w1s[0:F, :], ident[0:F, 0:F]).then_inc(S["w1_turned"], 1)
            pe.wait_ge(S["w1t_set"], 2)
            T.matmul(SETUP[0:F, 64:64 + F], w1t[0:64, :], w2s[0:64, :], start=True, stop=True)
            T.matmul(SETUP[:, 128:128 + F], b1b[0:64, :], w2s[0:64, :], start=True, stop=True).then_inc(S["w12_made"], 1)
            none = nil[:, 0:1].to_broadcast([P, HW])
            for k in range(2):
                T.matmul(bank[k][:, 0:HW], nil, none, start=True, stop=False)
            with pe.Fori(0, EB) as i:
                for b in range(2):
                    pe.wait_ge(S["h_ready"], i * 2 + (b + 1))

                    def turn(n):
                        k = i * (2 * NQ) + (b * NQ + n)
                        pe.wait_ge(S["hT_copied"], k + 1)
                        T.transpose(bank[5][:, 0:P], flat(ta)[:, n * P:(n + 1) * P], ident[:, :]).then_inc(S["h_turned"], 1)
                        pe.wait_ge(S["same_set"], k + 1)
                        for t in range(QW):
                            j = n * QW + t
                            last = T.transpose(bank[4][:, t * P:(t + 1) * P], srcc[b][:, j:j + 1].to_broadcast([P, P]), ident[:, :])
                        last.then_inc(S["src_turned"], 1)

                    def y(n, t):
                        k4 = i * (8 * NQ) + (4 * (b * NQ + n) + t)
                        pe.wait_ge(S["y_used"], k4 + 1)
                        T.matmul(bank[2 + t % 2][:, :], hT[(b * NQ + n) % 2][F * t:F * t + F, :], w0r[F * t:F * t + F, :],
                                 start=True, stop=True).then_inc(S["y_ready"], 1)

                    turn(0)
                    for n in range(NQ):
                        k = i * (2 * NQ) + (b * NQ + n)
                        pe.wait_ge(S["hT_copied"], k + 2)
                        y(n, 0)
                        y(n, 1)
                        for t in range(QW):
                            pe.wait_ge(S["hot_ready"], i * (8 * NQ) + (4 * (b * NQ + n) + t + 1))
                            for h in range(2):
                                last = T.matmul(bank[h][:, 0:HW], hotp[:, t, :], hot[t % 2][:, h * HW:(h + 1) * HW],
                                                start=False, stop=False)
                            last.then_inc(S["hot_used"], 1)
                            if t + 2 < QW:
                                y(n, t + 2)
                        if n + 1 < NQ:
                            turn(n + 1)
                        pe.wait_ge(S["msg_ready"], k + 1)
                        pe.wait_ge(S["sums_copied"], k + 1)
                        for t in range(QW):
                            last = T.matmul(bank[6][:, t * TW:(t + 1) * TW], s4[:, t, :], msg[:, t, :], start=True, stop=True)
                        last.then_inc(S["sum_ready"], 1)
            for k in range(2):
                last = T.matmul(bank[k][:, 0:HW], nil, none, start=False, stop=True)
            last.then_inc(S["hist_done"], 1)
            pe.wait_ge(S["tot_ready"], 1)
            T.matmul(SETUP[:, 0:NCH], after, ntot, start=True, stop=True)
            T.matmul(SETUP[:, NCH:2 * NCH], ones, ntot, start=True, stop=True).then_inc(S["offsets_made"], 1)

            def product(st, n, parts):
                pe.wait_ge(S[f"v_ready_{st}"], n + 1)
                for (v, _), tp in zip(parts, (T0, T1)):
                    for m in range(NQ):
                        last = T.transpose(tp[:, m * P:(m + 1) * P], flat(v)[:, m * P:(m + 1) * P], ident[:, :])
                last.then_inc(S[f"v_turned_{st}"], 1)
                pe.wait_ge(S[f"v_copied_{st}"], n + 1)
                for m in range(NQ):
                    for k, (_, w) in enumerate(parts):
                        last = T.matmul(U[:, m * P:(m + 1) * P], vT[k][:, m * P:(m + 1) * P], w[:, :],
                                        start=(k == 0), stop=(k == len(parts) - 1))
                last.then_inc(S[f"u_ready_{st}"], 1)

            def carry(q0, q):
                pe.wait_ge(S["ends_ready"], q)
                T.matmul(CARRY, link[:, :], ends[:, :], start=True, stop=True).then_inc(S["carry_ready"], 1)

            carry(1, 1)
            pe.wait_ge(S["bd_loaded"], 16 * QW)
            with pe.Fori(0, EB) as i:
                for b in range(2):
                    product("q2", i * 2 + b, [(ta, bd12)])
            carry(2, 2)
            carry(3, 3)
            with pe.Fori(0, EB) as i:
                for b in range(2):
                    product("q4", i * 2 + b, [(su, bda), (ta, bdb)])
            carry(4, 4)

            def body(q0, q, i, side, n):
                if side == "n":
                    product("n", n * 2, [(su, bd12)])
                    product("n", n * 2 + 1, [(su, bda)])
                if side == "d":
                    product("d", n * 2, [(ta, bd12)])
                    product("d", n * 2 + 1, [(su, bda), (ta, bdb)])

            def layer3_pe():
                for q0, pairs, side in ((Q_N, SP_N // 2, "n"), (Q_D, 1, "d")):
                    with pe.Fori(0, pairs) as kk:
                        for h in range(2):
                            with pe.Fori(0, EB) as i:
                                body(q0 + h, None, i, side, kk * (2 * EB) + (i + h * EB))
                            carry(q0 + h, kk * 2 + (q0 + h))
                with pe.Fori(Q_D + 2, Q_LAST + 1) as q:
                    carry(None, q)

            layer3_pe()


_INS = ["x", "src", "dst", "edge_attr_2", "L0_gnn_weight", "L1_gnn_W1", "L1_gnn_b1", "L1_gnn_W2", "L1_gnn_b2",
        "L2_gnn_W", "L2_gnn_b"]


def kernel(**inputs):
    import numpy as np
    import concourse.bacc as bacc
    from concourse import mybir as mb
    from concourse.bass_utils import run_bass_kernel_spmd

    nc = bacc.Bacc("TRN2", target_bir_lowering=False, num_devices=1)
    arrays, args = {}, []
    for name in _INS:
        a = np.ascontiguousarray(inputs[name])
        arrays[f"in_{name}"] = a
        args.append(nc.dram_tensor(f"in_{name}", a.shape, mb.dt.from_np(a.dtype), kind="ExternalInput").ap())
    shape = arrays["in_x"].shape
    args.append(nc.dram_tensor("out_x", shape, mb.dt.float32, kind="ExternalOutput").ap())
    gnn_stack(nc, *args)
    return run_bass_kernel_spmd(nc, [arrays], core_ids=[0]).results[0]["out_x"]
```

```python
import concourse.bass as bass
from concourse import mybir
from contextlib import ExitStack

P = 128
CW = 28
F = 32
QW = 4
NQ = CW // QW
NTAB = 2
TW = F + 1
NW = 36
PASSES = 10
ALPHA = 0.1
EPS = 1e-5


def gnn_stack(nc, x, src, dst, attr, w0, w1, b1, w2, b2, wl, bl, out):
    f32, i32, f16, bf16, u8 = (mybir.dt.float32, mybir.dt.int32, mybir.dt.float16, mybir.dt.bfloat16,
                               mybir.dt.uint8)
    ALU, ACT, AX = mybir.AluOpType, mybir.ActivationFunctionType, mybir.AxisListType

    N, E = x.shape[0], src.shape[0]
    CH = P * CW
    EC = -(-E // (2 * CH)) * 2 * CW
    ECH = EC // CW
    EB = ECH // 2
    NCH = -(-N // (2 * CH)) * 2
    NCOL = NCH * CW
    HW = NCOL // 2
    EP, NP = P * EC, P * NCOL
    ZROW = EP + P
    SRC_PAD, DST_PAD = N + P, N + P + 1
    EFULL, ETAIL = E // EC, E % EC
    NFULL, NREM = N // CH, N % CH
    NPF, NTAIL = NREM // CW, NREM % CW
    assert NP > DST_PAD and 0 < ETAIL and EFULL < P and HW <= 512 and NFULL == NCH - 1
    ES = CW * F
    OH = (NQ // 2 + 1) * QW
    GI = 16 * CW

    ctx = ExitStack()
    with ctx:
        def sb(name, shape, dt=f32):
            return ctx.enter_context(nc.sbuf_tensor(name, shape, dt))

        def sem(name):
            return ctx.enter_context(nc.semaphore(name))

        def dram(name, shape):
            return nc.dram_tensor(name, shape, f32, kind="Internal").ap()

        agg0 = [dram(f"agg0_{k}", (NP, TW)) for k in range(NTAB)]
        nodes = dram("nodes", (NP, NW))
        dst_rows = dram("dst_rows", (P, EC))
        placed = dram("placed", (EP, 4))
        run1, run2, run3, run4a, run4b = [dram(f"run_{n}", (EP + P + 1, F)) for n in ("1", "2", "3", "4a", "4b")]

        srci = sb("srci", [P, EC], i32)
        dsti = sb("dsti", [P, EC], i32)
        keep = sb("keep", [P, EC + 1])
        start = sb("start", [P, EC])
        startend = sb("startend", [P, EC])
        keepx = sb("keepx", [P, ECH, ES], u8)
        rowi = sb("rowi", [P, EC], i32)
        outi = sb("outi", [P, EC], i32)
        coefS = sb("coefS", [P, 5, EC])
        coefD = sb("coefD", [P, 5, EC])
        g36 = [sb(f"g36_{b}", [P, CW, NW]) for b in range(2)]
        gbuf = [t[:, :, :].rearrange("p c w -> p (c w)")[:, 0:ES].rearrange("p (c e) -> p c e", e=F) for t in g36]
        ident = sb("ident", [P, P])
        link = sb("link", [P, P])
        bd12, bda, bdb = [sb(n, [P, P]) for n in ("bd12", "bda", "bdb")]
        b12, b12n, b2r, blr = [sb(n, [P, F]) for n in ("b12", "b12n", "b2r", "blr")]
        firstrun, frpart, bound, ends = [sb(n, [P, F]) for n in ("firstrun", "frpart", "bound", "ends")]
        carries = sb("carries", [P, 4, F])
        small = sb("small", [P, 6, CW])
        ii = [sb(f"ii{b}", [P, CW], i32) for b in range(2)]
        di = sb("di", [P, CW], i32)
        epsc = sb("epsc", [P, 1])
        zrow = sb("zrow", [1, F])

        def flatc(t):
            return t.rearrange("p c e -> p (c e)")

        BIGW = 2 * EC * F if EC >= 10 * CW else 26 * EC + 8 * NCOL + 2 * NTAB * CW * TW + 2 * ES + 2048 + 128 * F
        big = sb("big", [P, BIGW])
        work = sb("work", [P, 14 * ES + CW * NW])

        def cutter(region):
            at = [0]

            def cut(n, dt=None):
                v = region[:, at[0]:at[0] + n]
                at[0] += n
                assert at[0] <= region.shape[1], at[0]
                return v.bitcast(dt) if dt is not None else v
            return cut

        def rm(t):
            return t.rearrange("p (c e) -> p c e", e=F)

        xs = rm(big[:, 0:EC * F])
        hs = rm(big[:, EC * F:2 * EC * F])
        xd = xs
        cut = cutter(work)
        mff = cut(ES)
        mf = mff.rearrange("p (f j) -> p f j", j=CW)
        mfr = mff.rearrange("p (f j) -> p j f", j=CW)
        rff = [cut(ES) for _ in range(2)]
        rf = [t.rearrange("p (f j) -> p f j", j=CW) for t in rff]
        ro = [rm(cut(ES)) for _ in range(2)]
        ta, tb, tc = [rm(cut(ES)) for _ in range(3)]
        vT = [cut(ES) for _ in range(2)]
        su = rm(cut(ES))
        sr = [rm(cut(ES)) for _ in range(3)]
        sx = cut(CW * NW).rearrange("p (c w) -> p c w", w=NW)
        dx = (coefS[:, 1:5, :].rearrange("p k c -> p (k c)")[:, 0:CW * NW] if 4 * EC >= CW * NW
              else sb("dx", [P, CW * NW])[:, :]).rearrange("p (c w) -> p c w", w=NW)
        lcut = cutter(work)
        ms = [lcut(CW * TW).rearrange("p (c w) -> p c w", w=TW) for _ in range(2)]
        dup = lcut(CW)
        oi = [lcut(CW, i32) for _ in range(2)]
        pad_to = lcut(CW)
        srcc = [lcut(CW) for _ in range(2)]
        hot = lcut(4 * HW, bf16).rearrange("p (t q) -> p t q", t=QW)
        msg = [lcut(QW * TW).rearrange("p (t w) -> p t w", w=TW) for _ in range(2)]
        nil = lcut(P // 2, bf16)
        lcut(5 * ES - 2 * CW * TW - 6 * CW - 4 * HW - 2 * QW * TW - P // 2)
        lcut(3 * ES)
        same = [lcut(QW * P) for _ in range(2)]
        s4 = [t.rearrange("p (t q) -> p t q", t=QW) for t in same]
        s1 = lcut(QW * P)
        zT = [lcut(4 * P) for _ in range(2)]
        hotp = lcut(QW * P // 2, bf16).rearrange("p (t q) -> p t q", t=QW)
        bcut = cutter(big)
        basis = bcut(16 * EC).rearrange("p (c k) -> p c k", k=16)
        attr_s = bcut(2 * EC)
        srcf, dstf, wpart, wfree, e1, e2, e3 = [bcut(EC) for _ in range(7)]
        ei = bcut(EC, i32)
        after, before, ones, iotar = [bcut(P) for _ in range(4)]
        iotaw = bcut(NCOL)
        iotan = bcut(HW, f16)
        cuts = bcut(NCOL)
        w0r = bcut(4 * F).rearrange("p (m o) -> p m o", m=4)
        zz = [bcut(QW * 16 * F).rearrange("p (t k f) -> p t k f", t=QW, f=F) for _ in range(2)]
        w1s, w2s, w1t, w12, b1b = bcut(64), bcut(F), bcut(F), bcut(F), bcut(P)
        b1c, pcol, dnext = bcut(1), bcut(1), bcut(1, i32)
        disorder, isunordered, rowcount = bcut(1), bcut(1, i32), bcut(1)
        later = bcut(1)
        rowno, partno = bcut(P, i32), bcut(1, i32)
        tents = work[:, 8 * ES:8 * ES + 8 * EC].rearrange("p (h c k) -> p h c k", h=2, k=4)
        keepc = wpart
        ncut = cutter(big[:, 0:18 * EC]) if 18 * EC >= NTAB * CW * TW + 2 * ES else bcut
        ndeg, nrow, n1, n2, n3 = [bcut(NCOL) for _ in range(5)]
        ni = bcut(NCOL, i32)
        ntot, nexc = bcut(NCH), bcut(NCH)
        aggb = [[c(CW * TW).rearrange("p (c w) -> p c w", w=TW) for _ in range(NTAB)] for c in (bcut, ncut)]
        xb = [rm(ncut(ES)) for _ in range(2)]

        pack = zz[0].rearrange("p t k f -> p (t k f)")[:, 0:4 * EC].rearrange("p (c k) -> p c k", k=4)
        g36f = flatc(g36[0][:, :, :])
        stage = g36f[:, 0:4 * CW].rearrange("p (c k) -> p c k", k=4)
        RB = 7
        cmp_ = work[:, 8 * ES:8 * ES + RB * EC].rearrange("p (t c) -> p t c", t=RB)
        other, bound_of = wpart, wfree
        rank, part_rank = e1, e3
        assert EC % RB == 0 and NCOL >= EC

        psum = ctx.enter_context(nc.psum_tensor("psum", [P, 8 * 512], f32))
        bank = [psum[:, 512 * k:512 * (k + 1)] for k in range(8)]
        T0, U, T1 = [psum[:, 1024 * k:1024 * k + ES] for k in range(3)]
        CARRY = bank[6][:, 0:F]
        SETUP = bank[7]

        names = """disorder_counted disorder_summed order_known rows_kept other_loaded other_used rank_ready stage_set
            edges_placed edges_reloaded filled loaded attr_loaded w_loaded bd_loaded zeroed before_added zrow_written
            iota_set matrices_set dst0_turned link_set count_carry keepc_set keepx_set roots_asked roots_set
            w1_turned w1t_set w12_made w12_set rows_set
            consumed idx_copied srcc_set src_turned same_set hot_ready hot_used z_ready z_used z_turned zT_copied
            msg_made msg_ready sum_ready sums_copied oi_ready hist_done tot_ready offsets_made
            node_asked node_made
            scanned run_copied ends_ready carry_ready bound_ready bound_written
            side_in sums_in side_gathered side_idx side_taken side_made side_written
            pool_passed d_taken fin_taken fin_made fin_idx""".split()
        names += [f"{n}{b}" for n in ("gathered", "run_written", "agg_loaded", "node_written", "fin_loaded",
                                      "scattered") for b in range(2)]
        names += [f"{n}_{st}" for n in ("ln_asked", "ln_done") for st in ("l0", "q1", "q3", "q4", "n", "d")]
        names += [f"{n}_{st}" for n in ("v_ready", "v_turned", "v_copied", "u_ready") for st in ("q2", "q4", "n", "d")]
        S = {n: sem(n) for n in names}
        added = [sem(f"added{k}") for k in range(NTAB)]
        SIDE_WRITTEN = 16 * (NFULL + (NPF > 0) + (NTAIL > 0)) + 1
        V, A, T = nc.vector, nc.scalar, nc.tensor

        def flat(t):
            return t.rearrange("p c e -> p (c e)")

        def edge_rows(table, c):
            t = table[0:EP, :].rearrange("(p c j) e -> p c (j e)", c=ECH, j=CW)
            return t[:, bass.ds(c, 1), :].rearrange("p a e -> p (a e)")

        def node_rows(table, c, n=NCH):
            t = table[0:n * CH, :].rearrange("(c p j) e -> p c (j e)", p=P, j=CW)
            return t[:, bass.ds(c, 1), :].rearrange("p a e -> p (a e)")

        def cols(t, c):
            s = bass.ds(c * CW, CW)
            return t[:, s] if len(t.shape) == 2 else t[:, s, :]

        def coef(t, k, c):
            return t[:, k, bass.ds(c * CW, CW)]

        def over_f(t):
            return t.unsqueeze(2).to_broadcast([P, CW, F])

        def over_c(t):
            return t.unsqueeze(1).to_broadcast([P, CW, F])

        def load_edges(q, tile, line, s, k=1):
            for a, z in ((0, EFULL // 16 * 16), (EFULL // 16 * 16, EFULL)):
                if z > a:
                    part = line[a * EC:z * EC] if k == 1 else line[a * EC:z * EC, :].rearrange("n k -> (n k)")
                    q.dma_start(tile[a:z, :], part.rearrange("(p c) -> p c", c=EC * k)).then_inc(s, 16)
            part = line[EFULL * EC:E] if k == 1 else line[EFULL * EC:E, :].rearrange("n k -> (n k)")
            q.dma_start(tile[EFULL:EFULL + 1, 0:ETAIL * k], part.rearrange("(a c) -> a c", a=1)).then_inc(s, 16)

        EDGE_DMAS = 1 + sum(z > a for a, z in ((0, EFULL // 16 * 16), (EFULL // 16 * 16, EFULL)))

        def step_of(q, i, b):
            return i * 2 + (q * ECH + b)

        def table_in(q):
            return {1: nodes, 2: run1, 3: run2, 4: run3}.get(q, run4a if q % 2 else run4b)

        def table_out(q):
            return {1: run1, 2: run2, 3: run3}.get(q, run4b if q % 2 else run4a)

        Q0, Q_LAST, HALF = 5, 3 + PASSES, (PASSES - 2) // 2
        Q1 = Q0 + HALF
        MID = min(2, EB)
        NA = -(-NCH // (2 * HALF))
        NB = (NCH - HALF * NA) // HALF
        DA = min(1, ECH // (3 * HALF))
        DB = (ECH - HALF * DA) // (HALF + 1)
        DL = ECH - HALF * (DA + DB)
        assert Q1 + HALF == Q_LAST and HALF % 2 == 0
        assert HALF * (NA + NB) == NCH and NA <= EB and DB <= 2 and DL <= 2 and (DB < 2 or MID <= EB - NB)

        def plan(half):
            return ((NA, 0, DA, 0), (NB, HALF * NA, DB, HALF * DA), (0, NCH, DL, ECH - DL))[half]

        def layer3(eng, dst, body, end=None, begin=None):
            def one(half, q0, q, k):
                nb, n0, m, d0 = plan(half)
                n = n0 + k * nb if nb else n0
                d = d0 + k * m if m else d0
                if m > 0:
                    dst(d, n)
                if begin:
                    begin(q0, q)
                cuts_at = [0] + ([MID] if m > 1 else []) + [EB - nb]
                for lo, hi in zip(cuts_at, cuts_at[1:]):
                    if lo:
                        dst(d + 1, n)
                    if hi > lo:
                        with eng.Fori(lo, hi) as i:
                            body(q0, q, i, None)
                if nb:
                    with eng.Fori(EB - nb, EB) as i:
                        body(q0, q, i, n + (i - (EB - nb)))
                if end:
                    end(q0, q)

            for half in range(2):
                with eng.Fori(0, HALF // 2) as kk:
                    for h in range(2):
                        q0 = Q0 + half * HALF + h
                        one(half, q0, kk * 2 + q0, kk * 2 + h)
            one(2, Q_LAST, Q_LAST, 0)

        block = ctx.enter_context(nc.Block())

        @block.sync
        def _(sp):
            sp.wait_ge(S["filled"], 1)
            load_edges(sp, dsti[:, :], dst, S["loaded"])
            load_edges(sp, srci[:, :], src, S["loaded"])
            with nc.allow_non_contiguous_dma(reason="one value of each partition"):
                sp.dma_start(dnext[0:EFULL, :], dst[EC:EC + (EFULL - 1) * EC + 1:EC].rearrange("(p a) -> p a", a=1))\
                  .then_inc(S["loaded"], 16)
            sp.wait_ge(S["filled"], 2)
            load_edges(sp, attr_s, attr, S["attr_loaded"], 2)
            sp.dma_start(w1s[0:F, :], w1).then_inc(S["w_loaded"], 16)
            sp.dma_start(w2s[0:64, :], w2).then_inc(S["w_loaded"], 16)
            with nc.allow_non_contiguous_dma(reason="a bias down the partitions"):
                sp.dma_start(b1c[0:64, :], b1.rearrange("(p a) -> p a", a=1)).then_inc(S["w_loaded"], 16)
            sp.dma_start(b2r[:, :], b2.rearrange("(a f) -> a f", a=1).to_broadcast([P, F])).then_inc(S["w_loaded"], 16)
            sp.dma_start(blr[:, :], bl.rearrange("(a f) -> a f", a=1).to_broadcast([P, F])).then_inc(S["w_loaded"], 16)
            for t in range(QW):
                r = slice(F * t, F * t + F)
                sp.dma_start(bda[r, r], wl[0:F, :]).then_inc(S["w_loaded"], 16)
                sp.dma_start(bdb[r, r], wl[F:2 * F, :]).then_inc(S["w_loaded"], 16)
            sp.dma_start(w0r, w0.rearrange("a b f o -> (a b f) o").rearrange("(m p) o -> p m o", p=P)).then_inc(S["w_loaded"], 16)
            for r in (run1, run2, run3, run4a, run4b):
                sp.dma_start(r[ZROW:ZROW + 1, :], zrow[:, :]).then_inc(S["zrow_written"], 16)
            with sp.Fori(1, NCH) as c:
                for k in range(NTAB):
                    sp.dma_start(node_rows(agg0[k], c), flat(ms[1])).then_inc(S["zeroed"], 16)
            sp.wait_ge(S["order_known"], 1)
            with sp.If(sp.value_load(isunordered[0:1, 0:1], min_val=0, max_val=EP) > 0):
                sp.dma_start(dst_rows, dstf).then_inc(S["rows_kept"], 16)
                sp.wait_ge(S["rows_kept"], 16)
                with sp.Fori(0, P) as r:
                    sp.wait_ge(S["other_used"], r + 1)
                    sp.dma_start(other, dst_rows[bass.ds(r, 1), :].to_broadcast([P, EC])).then_inc(S["other_loaded"], 16)
                sp.wait_ge(S["edges_placed"], GI * ECH)
                sp.dma_start(pack.rearrange("p c k -> p (c k)"), placed.rearrange("(p c) k -> p (c k)", p=P))\
                  .then_inc(S["edges_reloaded"], 16)
                with nc.allow_non_contiguous_dma(reason="one value of each partition"):
                    sp.dma_start(later[0:EFULL, :], placed[EC:EC + (EFULL - 1) * EC + 1:EC, 0:1])\
                      .then_inc(S["edges_reloaded"], 16)
            sp.wait_ge(S["w12_set"], 1)
            for t in range(QW):
                r = slice(F * t, F * t + F)
                sp.dma_start(bd12[r, r], w12[0:F, :]).then_inc(S["bd_loaded"], 16)

            for k in range(NTAB):
                sp.wait_ge(added[k], 16 + 16 * (EC // NTAB))

            def node_body(i, last):
                for b in range(2):
                    sp.wait_ge(S["node_asked"], i * 2 + (b + 1))
                    for k in range(NTAB):
                        sp.dma_start(flat(aggb[b][k]), node_rows(agg0[k], i * 2 + b)).then_inc(S[f"agg_loaded{b}"], 16)
                    s = S[f"agg_loaded{b}"]
                    if not (last and b):
                        sp.dma_start(flat(xb[b]), node_rows(x, i * 2 + b, NFULL)).then_inc(s, 16)
                    else:
                        if NPF:
                            lo = NFULL * CH
                            sp.dma_start(flat(xb[b][0:NPF]), x[lo:lo + NPF * CW, :].rearrange("(p j) e -> p (j e)", j=CW))\
                              .then_inc(s, 16)
                        if NTAIL:
                            lo = NFULL * CH + NPF * CW
                            sp.dma_start(flat(xb[b][NPF:NPF + 1, 0:NTAIL]), x[lo:N, :].rearrange("(p j) e -> p (j e)", p=1))\
                              .then_inc(s, 16)

            if NCH > 2:
                with sp.Fori(0, NCH // 2 - 1) as i:
                    node_body(i, False)
            node_body(NCH // 2 - 1, True)

            def write_runs(q0, q, i):
                for b in range(2):
                    sp.wait_ge(S["run_copied"], q * ECH + (i * 2 + (b + 3 - ECH)))
                    sp.dma_start(edge_rows(table_out(q0), i * 2 + b), flat(ro[b])).then_inc(S[f"run_written{b}"], 16)

            def write_bound(q0, q):
                sp.wait_ge(S["bound_ready"], q)
                sp.dma_start(table_out(q0)[EP:EP + P, :], bound[:, :]).then_inc(S["bound_written"], 16)

            for q in range(1, 5):
                with sp.Fori(0, EB) as i:
                    write_runs(q, q, i)
                write_bound(q, q)

            def side_in(n):
                sp.wait_ge(S["side_taken"], n + 1)
                sp.dma_start(flat(sx), node_rows(nodes, n)).then_inc(S["side_in"], 16)

            def side_out(n):
                sp.wait_ge(S["side_made"], n + 1)
                sp.dma_start(node_rows(out, n, NFULL), flat(su)).then_inc(S["side_written"], 16)

            def side_out_last():
                sp.wait_ge(S["side_made"], NCH)
                lo = NFULL * CH
                if NPF:
                    sp.dma_start(out[lo:lo + NPF * CW, :].rearrange("(p j) e -> p (j e)", j=CW), flat(su[0:NPF]))\
                      .then_inc(S["side_written"], 16)
                if NTAIL:
                    lo += NPF * CW
                    sp.dma_start(out[lo:N, :].rearrange("(p j) e -> p (j e)", p=1), flat(su[NPF:NPF + 1, 0:NTAIL]))\
                      .then_inc(S["side_written"], 16)

            def sums_in(d):
                sp.wait_ge(S["d_taken"], d + 1)
                for k, table in enumerate((run1, run2, run3)):
                    sp.dma_start(flat(sr[k]), edge_rows(table, d)).then_inc(S["sums_in"], 16)

            for q in range(Q0, Q_LAST + 1):
                half, k = divmod(q - Q0, HALF)
                nb, n0, m, d0 = plan(half)
                if m > 0:
                    sums_in(d0 + k * m)
                cuts_at = [0] + ([MID] if m > 1 else []) + [EB - nb]
                for lo, hi in zip(cuts_at, cuts_at[1:]):
                    if lo:
                        sums_in(d0 + k * m + 1)
                    if hi > lo:
                        with sp.Fori(lo, hi) as i:
                            write_runs(q, q, i)
                last = nb > 0 and n0 + k * nb + nb == NCH
                if nb > last:
                    with sp.Fori(EB - nb, EB - last) as i:
                        n = i + (n0 + k * nb - (EB - nb))
                        side_in(n)
                        side_out(n)
                        write_runs(q, q, i)
                if last:
                    side_in(NCH - 1)
                    side_out_last()
                    write_runs(q, q, EB - 1)
                write_bound(q, q)
            for b in range(2):
                sp.wait_ge(S[f"run_written{b}"], 16 * EB * Q_LAST + 1)
            sp.wait_ge(S["d_taken"], ECH + 1)
            with sp.Fori(0, EB) as i:
                for b in range(2):
                    sp.wait_ge(S["fin_taken"], i * 2 + (b + 1))
                    sp.dma_start(flat(sr[b]), edge_rows(table_out(Q_LAST), i * 2 + b)).then_inc(S[f"fin_loaded{b}"], 16)
            sp.wait_ge(S["bound_written"], 16 * Q_LAST)
            for b in range(2):
                sp.wait_ge(S[f"scattered{b}"], GI * EB)

        @block.gpsimd
        def _(pool):
            def wait(s, value):
                pool.wait_ge(s, value)
                pool.sem_inc(S["pool_passed"], 1)

            nc.gpsimd.iota(rowno, pattern=[[1, P]], base=0, channel_multiplier=0).then_inc(S["iota_set"], 1)
            nc.gpsimd.iota(ni[:, :], pattern=[[1, NCOL]], base=0, channel_multiplier=0).then_inc(S["iota_set"], 1)
            nc.gpsimd.iota(partno, pattern=[[0, 1]], base=0, channel_multiplier=1).then_inc(S["iota_set"], 1)
            nc.gpsimd.memset(ident[:, :], 0.0).then_inc(S["iota_set"], 1)
            wait(S["iota_set"], 4)
            nc.gpsimd.affine_select(out=ident[:, :], in_=ident[:, :], compare_op=ALU.not_equal, fill=1.0, base=0,
                                    pattern=[[-1, P]], channel_multiplier=1).then_inc(S["iota_set"], 1)

            def index_copied(index, q, i, b):
                g = step_of(q, i, b)
                wait(S["consumed"], g + 1)
                nc.gpsimd.tensor_copy(ii[b][:, :], cols(index, i * 2 + b)).then_inc(S["idx_copied"], 1)
                wait(S["idx_copied"], g + 1)

            def gather_column(table, w, b, j):
                o = g36[b][:, j, :] if w == NW else gbuf[b][:, j, :]
                pool.indirect_dma_start(o, None, table, bass.IndirectOffsetOnAxis(ii[b][:, j:j + 1], 0))\
                    .then_inc(S[f"gathered{b}"], 16)

            def gather(table, w, index, q, i, b):
                index_copied(index, q, i, b)
                for j in range(CW):
                    gather_column(table, w, b, j)

            def add_column(i, b, j):
                if j in (0, OH):
                    wait(S["oi_ready"], i * 4 + (2 * b + 1 + (j > 0)))
                if j % QW == 0:
                    wait(S["sums_copied"], i * 2 * NQ + (b * NQ + j // QW + 2))
                k = j % NTAB
                wait(added[k], i * (32 * CW // NTAB) + (16 + 16 * ((b * CW + j) // NTAB)))
                pool.indirect_dma_start(agg0[k], bass.IndirectOffsetOnAxis(oi[b][:, j:j + 1], 0), ms[b][:, j, :],
                                        None, compute_op=ALU.add).then_inc(added[k], 16)
                if j == NTAB - 1:
                    pool.sem_inc(S["before_added"], 1)

            wait(S["filled"], 2)
            for k in range(NTAB):
                pool.dma_start(node_rows(agg0[k], 0), flat(ms[1])).then_inc(added[k], 16)
            wait(S["order_known"], 1)
            with pool.If(pool.value_load(isunordered[0:1, 0:1], min_val=0, max_val=EP) > 0):
                wait(S["rank_ready"], 1)
                with pool.Fori(0, ECH) as c:
                    nc.gpsimd.tensor_copy(ii[0][:, :], cols(ei, c)).then_inc(S["stage_set"], 1)
                    nc.gpsimd.tensor_copy(stage, cols(pack, c)).then_inc(S["stage_set"], 1)
                    wait(S["stage_set"], c * 2 + 2)
                    for j in range(CW):
                        pool.indirect_dma_start(placed, bass.IndirectOffsetOnAxis(ii[0][:, j:j + 1], 0), stage[:, j, :], None)\
                            .then_inc(S["edges_placed"], 16)
                    wait(S["edges_placed"], c * GI + GI)
            wait(S["rows_set"], 1)
            for b in range(2):
                gather(x, F, rowi, 0, 0, b)
            wait(S["zeroed"], 16 * NTAB * (NCH - 1))
            if EB > 1:
                with pool.Fori(0, EB - 1) as i:
                    for b in range(2):
                        index_copied(rowi, 0, i + 1, b)
                        for j in range(CW):
                            gather_column(x, F, b, j)
                            add_column(i, b, j)
            for b in range(2):
                for j in range(CW):
                    add_column(EB - 1, b, j)

            for b in range(2):
                wait(S[f"node_written{b}"], 16 * (NCH // 2) + 1)
            with pool.Fori(0, EB) as i:
                for b in range(2):
                    gather(nodes, NW, srci, 1, i, b)

            def table_whole(q):
                for b in range(2):
                    wait(S[f"run_written{b}"], (q - 1) * (16 * EB) + 1)
                wait(S["bound_written"], (q - 1) * 16)

            wait(S["zrow_written"], 16 * 5)
            for q in range(2, 5):
                table_whole(q)
                with pool.Fori(0, EB) as i:
                    for b in range(2):
                        gather(table_in(q), F, rowi, q, i, b)

            def dst(d, n):
                wait(S["d_taken"], d + 1)
                nc.gpsimd.tensor_copy(di[:, :], cols(dsti, d)).then_inc(S["side_idx"], 1)
                wait(S["side_idx"], d + 1)
                for j in range(CW):
                    pool.indirect_dma_start(dx[:, j, :], None, nodes, bass.IndirectOffsetOnAxis(di[:, j:j + 1], 0))\
                        .then_inc(S["side_gathered"], 16)

            def body(q0, q, i, n):
                for b in range(2):
                    gather(table_in(q0), F, rowi, q, i, b)

            wait(S["scanned"], 4 * ECH)
            layer3(pool, dst, body, begin=lambda q0, q: table_whole(q))

            wait(S["side_written"], SIDE_WRITTEN)
            with pool.Fori(0, EB) as i:
                for b in range(2):
                    wait(S["fin_made"], i * 2 + (b + 1))
                    nc.gpsimd.tensor_copy(ii[b][:, :], cols(outi, i * 2 + b)).then_inc(S["fin_idx"], 1)
                    wait(S["fin_idx"], i * 2 + (b + 1))
                    for j in range(CW):
                        pool.indirect_dma_start(out, bass.IndirectOffsetOnAxis(ii[b][:, j:j + 1], 0), ro[b][:, j, :], None,
                                                bounds_check=N - 1, oob_is_err=False).then_inc(S[f"scattered{b}"], 16)

        @block.vector
        def _(dve):
            def dr():
                nc.vector.drain()

            def floordiv(xv, d, qv, r, t, ti):
                V.tensor_scalar(ti, xv, 1.0 / d, None, ALU.mult)
                dr()
                V.tensor_copy(qv, ti)
                dr()
                V.scalar_tensor_tensor(r, qv, -float(d), xv, ALU.mult, ALU.add)
                dr()
                V.tensor_scalar(t, r, 0.0, None, ALU.is_lt)
                dr()
                V.tensor_tensor(qv, qv, t, ALU.subtract)
                V.scalar_tensor_tensor(r, t, float(d), r, ALU.mult, ALU.add)
                dr()
                V.tensor_scalar(t, r, float(d), None, ALU.is_ge)
                dr()
                V.tensor_tensor(qv, qv, t, ALU.add)
                V.scalar_tensor_tensor(r, t, -float(d), r, ALU.mult, ALU.add)
                dr()

            dve.sem_inc(S["consumed"], 2)
            dve.sem_inc(S["hot_used"], QW)
            dve.sem_inc(S["msg_ready"], 1)
            for s in ("before_added", "run_written0", "run_written1", "node_written0", "node_written1", "other_used", "same_set", "sums_copied",
                      "side_taken", "d_taken", "side_written"):
                dve.sem_inc(S[s], 1)
            for s in ("sum_ready", "z_used", "zT_copied", "run_copied", "fin_taken", "node_asked"):
                dve.sem_inc(S[s], 2)
            V.memset(dsti[:, :], DST_PAD)
            V.memset(srci[:, :], SRC_PAD)
            dr()
            V.memset(dnext, DST_PAD).then_inc(S["filled"], 1)
            V.memset(attr_s, 0.0)
            V.memset(flat(ms[1]), 0.0)
            V.memset(zrow[:, :], 0.0)
            V.memset(epsc[:, :], EPS)
            for t in (bd12, bda, bdb):
                V.memset(t[:, :], 0.0)
            dr()
            V.memset(nil, 0.0).then_inc(S["filled"], 1)
            V.memset(ones, 1.0)
            for b in range(2):
                V.memset(msg[b][:, :, F:TW], 1.0)
            V.memset(cuts, 1.0)
            dr()
            V.memset(cuts.rearrange("p (c j) -> p c j", j=CW)[:, :, 0:1], 0.0)
            dve.wait_ge(S["iota_set"], 5)
            V.tensor_copy(iotar, rowno)
            V.tensor_copy(iotaw, ni)
            V.tensor_copy(pcol, partno)
            dr()
            V.tensor_copy(iotan, iotaw)
            V.tensor_scalar(after, iotar, pcol, None, ALU.is_gt)
            V.tensor_scalar(before, iotar, pcol, None, ALU.is_lt)
            dve.wait_ge(S["loaded"], 16 * (2 * EDGE_DMAS + 1))
            V.tensor_copy(dstf, dsti[:, :])
            V.tensor_copy(srcf, srci[:, :])
            V.tensor_copy(e2[:, 0:1], dnext)
            dr()
            V.tensor_tensor(e1[:, 1:EC], dstf[:, 1:EC], dstf[:, 0:EC - 1], ALU.is_lt)
            V.tensor_tensor(e1[:, 0:1], e2[:, 0:1], dstf[:, EC - 1:EC], ALU.is_lt)
            dr()
            V.tensor_reduce(disorder, e1, AX.X, ALU.add).then_inc(S["disorder_counted"], 1)
            dve.wait_ge(S["disorder_summed"], 1)
            V.tensor_copy(isunordered, SETUP[:, 0:1]).then_inc(S["order_known"], 1)
            dve.wait_ge(S["order_known"], 1)
            with dve.If(dve.value_load(isunordered[0:1, 0:1], min_val=0, max_val=EP) > 0):
                dve.wait_ge(S["attr_loaded"], 16 * EDGE_DMAS)
                V.tensor_copy(pack[:, :, 0], dstf)
                V.tensor_copy(pack[:, :, 1], srcf)
                V.tensor_copy(pack[:, :, 2:4], attr_s.rearrange("p (c k) -> p c k", k=2))
                V.memset(rank, 0.0)
                V.memset(rowcount, 0.0)
                dr()
                with dve.Fori(0, P) as r:
                    dve.wait_ge(S["other_loaded"], r * 16 + 16)
                    V.tensor_tensor(later, pcol, rowcount, ALU.is_gt)
                    dr()
                    V.tensor_scalar(bound_of, dstf, later, None, ALU.add)
                    dr()
                    with dve.Fori(0, EC // RB) as t:
                        V.tensor_tensor(cmp_, other.unsqueeze(1).to_broadcast([P, RB, EC]),
                                        bound_of[:, bass.ds(t * RB, RB)].unsqueeze(2).to_broadcast([P, RB, EC]), ALU.is_lt)
                        dr()
                        V.tensor_reduce(part_rank[:, bass.ds(t * RB, RB)], cmp_, AX.X, ALU.add)
                        dr()
                    V.tensor_tensor(rank, rank, part_rank, ALU.add)
                    V.tensor_scalar(rowcount, rowcount, 1.0, None, ALU.add)
                    dr()
                    dve.sem_inc(S["other_used"], 1)
                with dve.Fori(0, EC) as j:
                    V.tensor_scalar(cmp_[:, 0, :], iotaw[:, 0:EC], iotaw[:, bass.ds(j, 1)], None, ALU.is_lt)
                    dr()
                    V.scalar_tensor_tensor(cmp_[:, 1, :], dstf, dstf[:, bass.ds(j, 1)], cmp_[:, 0, :], ALU.is_equal, ALU.mult)
                    dr()
                    V.tensor_reduce(part_rank[:, bass.ds(j, 1)], cmp_[:, 1, :], AX.X, ALU.add)
                    dr()
                V.tensor_tensor(rank, rank, part_rank, ALU.add)
                V.memset(later, float(DST_PAD))
                dr()
                V.tensor_copy(ei, rank).then_inc(S["rank_ready"], 1)
                dve.wait_ge(S["edges_reloaded"], 32)
                V.tensor_copy(dstf, pack[:, :, 0])
                V.tensor_copy(srcf, pack[:, :, 1])
                V.tensor_copy(dnext, later)
                V.tensor_copy(attr_s.rearrange("p (c k) -> p c k", k=2), pack[:, :, 2:4])
                dr()
                V.tensor_copy(dsti[:, :], dstf)
                V.tensor_copy(srci[:, :], srcf)
                dr()
            V.tensor_scalar(e1, dstf, float(N - 1), None, ALU.min)
            dr()
            V.tensor_copy(rowi[:, :], e1).then_inc(S["rows_set"], 1)
            V.tensor_scalar(pad_to, pcol.to_broadcast([P, CW]), float(N), None, ALU.add)
            floordiv(dstf, CH, e1, e2, e3, ei)
            floordiv(e2, CW, wpart, wfree, e3, ei)
            V.scalar_tensor_tensor(wfree, e1, float(CW), wfree, ALU.mult, ALU.add)
            dve.wait_ge(S["attr_loaded"], 16 * EDGE_DMAS)
            av = attr_s.rearrange("p (c k) -> p c k", k=2)
            for h in range(2):
                for k in range(4):
                    V.tensor_scalar(tents[:, h, :, k], av[:, :, h], -float(-1.0 + k * (2.0 / 3.0)), None, ALU.add)
            dr()
            V.scalar_tensor_tensor(tents, tents, -1.0, tents, ALU.mult, ALU.max)
            dr()
            V.tensor_scalar(tents, tents, -1.5, 1.0, ALU.mult, ALU.add)
            dr()
            V.tensor_scalar(tents[:, 0], tents[:, 0], 0.0, None, ALU.max)
            dr()
            for m in range(4):
                V.scalar_tensor_tensor(basis[:, :, 4 * m:4 * m + 4], tents[:, 1], 0.0,
                                       tents[:, 0, :, m].unsqueeze(2).to_broadcast([P, EC, 4]), ALU.max, ALU.mult)
            dr()
            dve.wait_ge(S["w_loaded"], 16 * (6 + 2 * QW))
            V.tensor_copy(b1b[0:64, :], b1c[0:64, :].to_broadcast([64, P])).then_inc(S["w1t_set"], 1)
            dve.wait_ge(S["w1_turned"], 1)
            V.tensor_copy(w1t[0:64, :], SETUP[0:64, 0:F]).then_inc(S["w1t_set"], 1)
            dve.wait_ge(S["w12_made"], 1)
            V.tensor_copy(w12[0:F, :], SETUP[0:F, 64:64 + F]).then_inc(S["w12_set"], 1)
            V.tensor_copy(b12[:, :], SETUP[:, 128:128 + F])
            dr()
            V.tensor_tensor(b12n[:, :], b12[:, :], b2r[:, :], ALU.add)
            dr()

            def layernorm(st, n, xin, h, signal=None):
                V.tensor_reduce(small[:, 0, :], xin, AX.X, ALU.add)
                dr()
                V.tensor_scalar(small[:, 1, :], small[:, 0, :], -1.0 / F, None, ALU.mult)
                dr()
                ins = V.tensor_tensor(tb, xin, over_f(small[:, 1, :]), ALU.add)
                ins.then_inc(S[f"ln_asked_{st}"], 1)
                dve.wait_ge(S[f"ln_done_{st}"], n * 2 + 1)
                if signal:
                    dve.sem_inc(S[signal], 1)
                V.tensor_reduce(small[:, 2, :], tc, AX.X, ALU.add).then_inc(S[f"ln_asked_{st}"], 1)
                dve.wait_ge(S[f"ln_done_{st}"], n * 2 + 2)
                V.reciprocal(small[:, 4, :], small[:, 3, :])
                dr()
                return V.scalar_tensor_tensor(h, tb, 0.0, over_f(small[:, 4, :]), ALU.max, ALU.mult)

            def chunk_arrived(q, i, b):
                dve.wait_ge(S[f"gathered{b}"], (q * EB + i) * GI + GI)

            def layer0_chunk(i, b):
                g = i * 2 + b
                V.tensor_copy(srcc[b], cols(srcf, g)).then_inc(S["srcc_set"], 1)
                chunk_arrived(0, i, b)
                layernorm("l0", g, gbuf[b], ta, "consumed")
                dr()
                for n in range(NQ):
                    k = i * (2 * NQ) + (b * NQ + n)
                    par = (b * NQ + n) % 2
                    qc = bass.ds(i * (2 * CW) + (b * CW + n * QW), QW)
                    dve.wait_ge(S["z_used"], k + 1)
                    for t in range(QW):
                        col = i * (2 * CW) + (b * CW + n * QW + t)
                        last = V.tensor_tensor(
                            zz[par][:, t], ta[:, n * QW + t, :].unsqueeze(1).to_broadcast([P, 16, F]),
                            basis[:, bass.ds(col, 1), :].rearrange("p a k -> p (a k)").unsqueeze(2).to_broadcast([P, 16, F]),
                            ALU.mult)
                    last.then_inc(S["z_ready"], 1)
                    dve.wait_ge(S["sum_ready"], k + 1)
                    dve.wait_ge(S["src_turned"], k + 1)
                    V.tensor_tensor(s4[par], bank[4].rearrange("p (t q) -> p t q", t=QW),
                                    srcf[:, qc].unsqueeze(2).to_broadcast([P, QW, P]), ALU.is_equal)\
                        .then_inc(S["same_set"], 1)
                    dve.wait_ge(S["hot_used"], 4 * k + 4)
                    V.tensor_tensor(hotp, iotar.unsqueeze(1).to_broadcast([P, QW, P]),
                                    wpart[:, qc].unsqueeze(2).to_broadcast([P, QW, P]), ALU.is_equal)
                    dr()
                    for t in range(QW):
                        col = i * (2 * CW) + (b * CW + n * QW + t)
                        V.tensor_scalar(hot[:, t, :], iotan, wfree[:, bass.ds(col, 1)], None, ALU.is_equal)\
                            .then_inc(S["hot_ready"], 1)
                        V.tensor_tensor_reduce(out=s1[:, t * P:(t + 1) * P], in0=s4[par][:, t, :], in1=before, scale=1.0, scalar=0.0,
                                               op0=ALU.mult, op1=ALU.add, accum_out=dup[:, n * QW + t:n * QW + t + 1])
                    if n in (NQ // 2, NQ - 1):
                        lo, hi = (0, OH) if n == NQ // 2 else (OH, CW)
                        s5, sc = small[:, 5, lo:hi], srcf[:, bass.ds(i * (2 * CW) + (b * CW + lo), hi - lo)]
                        V.tensor_tensor(s5, pad_to[:, lo:hi], sc, ALU.subtract)
                        dr()
                        V.scalar_tensor_tensor(s5, dup[:, lo:hi], 1.0, s5, ALU.min, ALU.mult)
                        dr()
                        dve.wait_ge(S["before_added"], i * 2 + (b + 1))
                        V.tensor_tensor(oi[b][:, lo:hi], s5, sc, ALU.add).then_inc(S["oi_ready"], 1)

            with dve.Fori(0, EB) as i:
                for b in range(2):
                    layer0_chunk(i, b)

            dve.wait_ge(S["hist_done"], 1)
            V.tensor_copy(ndeg[:, 0:HW], bank[0][:, 0:HW])
            V.tensor_copy(ndeg[:, HW:NCOL], bank[1][:, 0:HW])
            dr()
            V.tensor_tensor_scan(n1, cuts, ndeg, 0.0, ALU.mult, ALU.add)
            dr()
            n1v = n1.rearrange("p (c j) -> p c j", j=CW)
            V.tensor_copy(ntot, n1v[:, :, CW - 1]).then_inc(S["tot_ready"], 1)
            dve.wait_ge(S["offsets_made"], 1)
            V.tensor_copy(n3[:, 0:NCH], SETUP[:, NCH:2 * NCH])
            dr()
            V.tensor_tensor_scan(nexc, ones[:, 0:NCH], n3[:, 0:NCH], 0.0, ALU.mult, ALU.add)
            dr()
            V.tensor_tensor(nexc, nexc, n3[:, 0:NCH], ALU.subtract)
            dr()
            V.tensor_tensor(nexc, nexc, SETUP[:, 0:NCH], ALU.add)
            dr()
            V.tensor_tensor(n1v, n1v, nexc.unsqueeze(2).to_broadcast([P, NCH, CW]), ALU.add)
            dr()
            V.tensor_scalar(n1, n1, -1.0, None, ALU.add)
            dr()
            floordiv(n1, EC, n2, n3, nrow, ni)
            V.tensor_tensor(nrow, n3, ndeg, ALU.is_lt)
            V.tensor_scalar(n2, n2, float(EP), None, ALU.add)
            dr()
            V.tensor_tensor(n2, n2, n1, ALU.subtract)
            dr()
            V.tensor_tensor(n2, n2, nrow, ALU.mult)
            dr()
            V.tensor_tensor(nrow, n2, n1, ALU.add)
            V.tensor_scalar(n3, ndeg, 1.0, None, ALU.min)
            dr()
            V.tensor_scalar(nrow, nrow, -float(ZROW), None, ALU.add)
            dr()
            V.tensor_tensor(nrow, nrow, n3, ALU.mult)
            dr()
            V.tensor_scalar(nrow, nrow, float(ZROW), None, ALU.add)
            for b in range(2):
                V.memset(g36[b][:, :, F + 3:NW], 0.0)
            dr()

            def node_chunk(i, b, loads):
                dve.wait_ge(S[f"agg_loaded{b}"], loads)
                dve.wait_ge(S[f"node_written{b}"], i * 16 + 1)
                a = aggb[b]
                V.tensor_tensor(a[0], a[0], a[1], ALU.add)
                dr()
                V.tensor_tensor(g36[b][:, :, 0:F], a[0][:, :, 0:F], xb[b], ALU.add)
                V.tensor_copy(g36[b][:, :, F], a[0][:, :, F])
                V.tensor_copy(g36[b][:, :, F + 1], cols(ndeg, i * 2 + b))
                V.tensor_copy(g36[b][:, :, F + 2], cols(nrow, i * 2 + b))
                dr()
                dve.sem_inc(S["node_asked"], 1)
                dve.sem_inc(S["node_made"], 1)

            PER = 16 * (NTAB + 1)
            if NCH > 2:
                with dve.Fori(0, NCH // 2 - 1) as i:
                    for b in range(2):
                        node_chunk(i, b, i * PER + PER)
            node_chunk(NCH // 2 - 1, 0, NCH // 2 * PER)
            node_chunk(NCH // 2 - 1, 1, NCH // 2 * PER - 16 + 16 * ((NPF > 0) + (NTAIL > 0)))

            V.memset(e3, 1.0)
            V.memset(keep[:, 0:1], 0.0)
            V.tensor_tensor(keep[:, 1:EC], dstf[:, 1:EC], dstf[:, 0:EC - 1], ALU.is_equal)
            V.tensor_copy(e2[:, 0:1], dnext)
            dr()
            V.tensor_tensor(keep[:, EC:EC + 1], dstf[:, EC - 1:EC], e2[:, 0:1], ALU.is_equal)
            V.tensor_scalar(start[:, :], dstf, dstf[:, 0:1], None, ALU.is_equal).then_inc(S["matrices_set"], 1)
            dr()
            V.tensor_tensor(startend[:, 0:EC - 1], start[:, 0:EC - 1], start[:, 1:EC], ALU.subtract)
            V.tensor_copy(startend[:, EC - 1:EC], start[:, EC - 1:EC])
            V.scalar_tensor_tensor(e1, keep[:, 1:EC + 1], float(1 << 20), dstf, ALU.mult, ALU.add)
            V.tensor_copy(keepc, keep[:, 0:EC])
            dr()
            V.memset(keepc.rearrange("p (c j) -> p c j", j=CW)[:, :, 0:1], 0.0).then_inc(S["keepc_set"], 1)
            V.tensor_copy(outi[:, :], e1)
            V.tensor_tensor_scan(e2, keep[:, 0:EC], e3, 0.0, ALU.mult, ALU.add)
            dve.wait_ge(S["dst0_turned"], 1)
            V.scalar_tensor_tensor(link[:, :], SETUP[:, 0:P], dstf[:, EC - 1:EC], after, ALU.is_equal, ALU.mult)\
                .then_inc(S["link_set"], 1)
            dve.wait_ge(S["count_carry"], 1)
            dr()
            V.tensor_copy(e1[:, 0:1], SETUP[:, 0:1])
            dr()
            V.scalar_tensor_tensor(e3, start[:, :], e1[:, 0:1], e2, ALU.mult, ALU.add)
            dr()
            V.tensor_scalar(e1, e3, 1.0, None, ALU.add)
            V.tensor_scalar(e2, e3, 1.0, None, ALU.max)
            dr()
            V.reciprocal(coefD[:, 0, :], e1)
            V.reciprocal(coefD[:, 1, :], e2).then_inc(S["roots_asked"], 1)
            dve.wait_ge(S["roots_set"], 2)
            V.reciprocal(coefD[:, 2, :], e1)
            V.reciprocal(coefD[:, 3, :], e2)
            tbf = flat(tb).rearrange("p (f j) -> p f j", j=CW)
            U3 = rm(U)
            for t in rff:
                V.memset(t, 0.0)
            V.memset(firstrun[:, :], 0.0)
            dve.wait_ge(S["bd_loaded"], 16 * QW)
            dve.wait_ge(S["keepx_set"], ECH)

            def scan_chunk(q, i, b):
                c = i * 2 + b
                g1 = q * ECH + (i * 2 + (b + 1 - ECH))
                V.scalar_tensor_tensor(mf[:, :, 0], rf[1 - b][:, :, CW - 1], keep[:, bass.ds(c * CW, 1)], mf[:, :, 0],
                                       ALU.mult, ALU.add)
                dr()
                dve.wait_ge(S["run_copied"], g1)
                V.tensor_tensor_scan(rff[b], keepx[:, bass.ds(c, 1), :].rearrange("p a e -> p (a e)"), mff, 0.0,
                                     ALU.mult, ALU.add).then_inc(S["scanned"], 1)
                dr()
                V.tensor_tensor(tbf, rf[b], cols(startend, c).unsqueeze(1).to_broadcast([P, F, CW]), ALU.mult)
                dr()
                V.tensor_reduce(frpart[:, :], tbf, AX.X, ALU.add)
                dr()
                V.tensor_tensor(firstrun[:, :], firstrun[:, :], frpart[:, :], ALU.add)
                dr()

            def pass_end(q0, q):
                if q0 > 1:
                    dve.wait_ge(S["bound_written"], q * 16 - 16)
                V.tensor_copy(ends[:, :], rf[1][:, :, CW - 1]).then_inc(S["ends_ready"], 1)
                dve.wait_ge(S["carry_ready"], q)
                V.tensor_copy(carries[:, min(q0 - 1, 3), :], CARRY)
                V.tensor_tensor(bound[:, :], firstrun[:, :], CARRY, ALU.add)
                dr()
                V.memset(firstrun[:, :], 0.0)
                dr()
                dve.sem_inc(S["bound_ready"], 1)

            def pass1(i, b):
                c = i * 2 + b
                chunk_arrived(1, i, b)
                g = g36[b]
                sl = bass.ds(c * CW, CW)
                V.tensor_copy(cols(rowi, c), g[:, :, F + 2])
                V.tensor_copy(cols(xs, c), g[:, :, 0:F])
                V.tensor_scalar(small[:, 0, :], g[:, :, F + 1], 1.0, None, ALU.add)
                V.tensor_scalar(small[:, 1, :], g[:, :, F + 1], 1.0, None, ALU.max)
                V.tensor_scalar(small[:, 2, :], g[:, :, F], 1.0, None, ALU.max)
                dr()
                dve.sem_inc(S["consumed"], 1)
                V.reciprocal(coefS[:, 0:2, sl], small[:, 0:2, :]).then_inc(S["roots_asked"], 1)
                dve.wait_ge(S["roots_set"], i * 2 + (b + 3))
                V.reciprocal(coefS[:, 2:5, sl], small[:, 0:3, :])
                dr()
                layernorm("q1", c, cols(xs, c), cols(hs, c))
                dr()
                V.tensor_tensor(mfr, cols(hs, c), over_f(coef(coefS, 2, c)), ALU.mult)
                dr()
                scan_chunk(1, i, b)

            with dve.Fori(0, EB) as i:
                for b in range(2):
                    pass1(i, b)
            pass_end(1, 1)

            def pass2(i, b):
                c = i * 2 + b
                chunk_arrived(2, i, b)
                V.tensor_tensor(ta, gbuf[b], over_f(coef(coefS, 2, c)), ALU.mult).then_inc(S["consumed"], 1)
                V.tensor_tensor(tb, cols(hs, c), over_f(coef(coefS, 0, c)), ALU.mult)
                dr()
                V.tensor_tensor(ta, ta, tb, ALU.add).then_inc(S["v_ready_q2"], 1)
                dve.wait_ge(S["u_ready_q2"], c + 1)
                V.tensor_tensor(cols(hs, c), U3, over_c(b12[:, :]), ALU.add)
                dr()
                V.tensor_tensor(mfr, cols(hs, c), over_f(coef(coefS, 2, c)), ALU.mult)
                dr()
                scan_chunk(2, i, b)

            with dve.Fori(0, EB) as i:
                for b in range(2):
                    pass2(i, b)
            pass_end(2, 2)

            def pass3(i, b):
                c = i * 2 + b
                chunk_arrived(3, i, b)
                V.tensor_tensor(ta, gbuf[b], over_f(coef(coefS, 2, c)), ALU.mult).then_inc(S["consumed"], 1)
                V.tensor_tensor(tb, cols(hs, c), over_f(coef(coefS, 0, c)), ALU.mult)
                dr()
                V.tensor_tensor(ta, ta, tb, ALU.add)
                dr()
                V.tensor_tensor(ta, ta, over_c(b2r[:, :]), ALU.add)
                dr()
                V.scalar_tensor_tensor(cols(xs, c), ta, 0.0, cols(xs, c), ALU.max, ALU.add)
                dr()
                layernorm("q3", c, cols(xs, c), cols(hs, c))
                dr()
                V.tensor_copy(mfr, cols(hs, c))
                dr()
                scan_chunk(3, i, b)

            with dve.Fori(0, EB) as i:
                for b in range(2):
                    pass3(i, b)
            pass_end(3, 3)

            def pass4(i, b):
                c = i * 2 + b
                chunk_arrived(4, i, b)
                V.tensor_tensor(ta, gbuf[b], over_f(coef(coefS, 1, c)), ALU.mult).then_inc(S["consumed"], 1)
                V.tensor_copy(su, cols(hs, c))
                dr()
                dve.sem_inc(S["v_ready_q4"], 1)
                dve.wait_ge(S["u_ready_q4"], c + 1)
                V.tensor_tensor(tb, U3, over_c(blr[:, :]), ALU.add)
                V.scalar_tensor_tensor(coef(coefS, 0, c), coef(coefS, 4, c), 1.0 - ALPHA, coef(coefS, 3, c), ALU.mult, ALU.mult)
                dr()
                V.scalar_tensor_tensor(cols(xs, c), tb, 0.0, cols(xs, c), ALU.max, ALU.add)
                dr()
                layernorm("q4", c, cols(xs, c), ta)
                dr()
                V.tensor_tensor(mfr, ta, over_f(coef(coefS, 4, c)), ALU.mult)
                dr()
                V.tensor_scalar(cols(hs, c), mfr, ALPHA, None, ALU.mult)
                dr()
                scan_chunk(4, i, b)

            with dve.Fori(0, EB) as i:
                for b in range(2):
                    pass4(i, b)
            pass_end(4, 4)

            sxx = sx[:, :, 0:F]

            def side_nodes(n):
                dve.wait_ge(S["side_in"], n * 16 + 16)
                dve.wait_ge(S["side_written"], n * 16 + 1)
                layernorm("n", n * 3, sxx, su).then_inc(S["v_ready_n"], 1)
                dve.wait_ge(S["u_ready_n"], n * 2 + 1)
                V.tensor_tensor(ta, U3, over_c(b12n[:, :]), ALU.add)
                dr()
                V.scalar_tensor_tensor(sxx, ta, 0.0, sxx, ALU.max, ALU.add)
                dr()
                layernorm("n", n * 3 + 1, sxx, su).then_inc(S["v_ready_n"], 1)
                dve.wait_ge(S["u_ready_n"], n * 2 + 2)
                V.tensor_tensor(ta, U3, over_c(blr[:, :]), ALU.add)
                dr()
                V.scalar_tensor_tensor(sxx, ta, 0.0, sxx, ALU.max, ALU.add)
                dr()
                layernorm("n", n * 3 + 2, sxx, ta)
                dr()
                V.scalar_tensor_tensor(su, ta, ALPHA, sxx, ALU.mult, ALU.add).then_inc(S["side_made"], 1)
                dr()
                dve.sem_inc(S["side_taken"], 1)

            def side_dst(n, nodes_before):
                sxx = dx[:, :, 0:F]
                dve.wait_ge(S["sums_in"], n * 48 + 48)
                dve.wait_ge(S["side_gathered"], n * GI + GI)
                all_before = isinstance(nodes_before, int) and nodes_before == NCH
                dve.wait_ge(S["side_written"], SIDE_WRITTEN if all_before else nodes_before * 16 + 1)

                def summed(k):
                    V.tensor_tensor(ta, over_f(cols(start, n)), over_c(carries[:, k, :]), ALU.mult)
                    dr()
                    V.tensor_tensor(ta, ta, sr[k], ALU.add)
                    dr()

                layernorm("d", n * 3, sxx, su)
                summed(0)
                V.tensor_tensor(ta, ta, over_f(coef(coefD, 2, n)), ALU.mult)
                V.tensor_tensor(tb, su, over_f(coef(coefD, 0, n)), ALU.mult)
                dr()
                V.tensor_tensor(ta, ta, tb, ALU.add).then_inc(S["v_ready_d"], 1)
                dve.wait_ge(S["u_ready_d"], n * 2 + 1)
                V.tensor_tensor(su, U3, over_c(b12[:, :]), ALU.add)
                summed(1)
                V.tensor_tensor(ta, ta, over_f(coef(coefD, 2, n)), ALU.mult)
                V.tensor_tensor(tb, su, over_f(coef(coefD, 0, n)), ALU.mult)
                dr()
                V.tensor_tensor(ta, ta, tb, ALU.add)
                dr()
                V.tensor_tensor(ta, ta, over_c(b2r[:, :]), ALU.add)
                dr()
                V.scalar_tensor_tensor(sxx, ta, 0.0, sxx, ALU.max, ALU.add)
                dr()
                layernorm("d", n * 3 + 1, sxx, su)
                summed(2)
                V.tensor_tensor(ta, ta, over_f(coef(coefD, 1, n)), ALU.mult).then_inc(S["v_ready_d"], 1)
                dve.wait_ge(S["u_ready_d"], n * 2 + 2)
                V.tensor_tensor(tb, U3, over_c(blr[:, :]), ALU.add)
                dr()
                V.scalar_tensor_tensor(sxx, tb, 0.0, sxx, ALU.max, ALU.add)
                dr()
                layernorm("d", n * 3 + 2, sxx, ta)
                dr()
                V.scalar_tensor_tensor(cols(xd, n), ta, ALPHA, sxx, ALU.mult, ALU.add)
                dr()
                dve.sem_inc(S["d_taken"], 1)

            def body(q0, q, i, n):
                if n is not None:
                    side_nodes(n)
                for b in range(2):
                    c = i * 2 + b
                    chunk_arrived(q, i, b)
                    V.tensor_tensor(mfr, gbuf[b], over_f(coef(coefS, 0, c)), ALU.mult).then_inc(S["consumed"], 1)
                    dr()
                    V.tensor_tensor(mfr, mfr, cols(hs, c), ALU.add)
                    dr()
                    scan_chunk(q, i, b)

            layer3(dve, side_dst, body, end=pass_end)

            for b in range(2):
                dve.wait_ge(S[f"run_written{b}"], 16 * EB * Q_LAST + 1)

            def final(i, b, first=False):
                c = i * 2 + b
                dve.wait_ge(S[f"fin_loaded{b}"], i * 16 + 16)
                V.tensor_tensor(ta, over_f(cols(start, c)), over_c(carries[:, 3, :]), ALU.mult)
                dr()
                V.tensor_tensor(ta, ta, sr[b], ALU.add).then_inc(S["fin_taken"], 1)
                dr()
                V.tensor_tensor(ta, ta, over_f(coef(coefD, 3, c)), ALU.mult)
                dr()
                if not first:
                    dve.wait_ge(S[f"scattered{b}"], i * GI)
                V.scalar_tensor_tensor(ro[b], ta, 1.0 - ALPHA, cols(xd, c), ALU.mult, ALU.add)\
                    .then_inc(S["fin_made"], 1)
                dr()

            for b in range(2):
                final(0, b, True)
            if EB > 1:
                with dve.Fori(1, EB) as i:
                    for b in range(2):
                        final(i, b)

        @block.scalar
        def _(act):
            def layernorm(st, n):
                act.wait_ge(S[f"ln_asked_{st}"], n * 2 + 1)
                A.activation(tc, tb, ACT.Square).then_inc(S[f"ln_done_{st}"], 1)
                act.wait_ge(S[f"ln_asked_{st}"], n * 2 + 2)
                A.activation(small[:, 3, :], small[:, 2, :], ACT.Sqrt, bias=epsc[:, 0:1], scale=1.0 / F)\
                    .then_inc(S[f"ln_done_{st}"], 1)

            def sums_copy(i, m):
                b, n = divmod(m, NQ)
                if n == 0:
                    act.wait_ge(S["before_added"], i * 2 + (b + 1))
                act.wait_ge(S["sum_ready"], i * (2 * NQ) + (m + 3))
                A.copy(ms[b][:, n * QW:(n + 1) * QW, :], bank[6][:, 0:QW * TW].rearrange("p (t w) -> p t w", w=TW))\
                    .then_inc(S["sums_copied"], 1)

            def layer0_body(i, first=False):
                for m in range(2 * NQ):
                    if m % NQ == 0:
                        layernorm("l0", i * 2 + m // NQ)
                    for t in range(QW):
                        act.wait_ge(S["z_turned"], i * (8 * NQ) + (4 * m + t + 1))
                        A.copy(zT[t % 2], bank[2 + t % 2]).then_inc(S["zT_copied"], 1)
                        if t == 1 and m:
                            if first and m == 1:
                                act.wait_ge(S["zeroed"], 16 * NTAB * (NCH - 1))
                                for k in range(NTAB):
                                    act.wait_ge(added[k], 16)
                            sums_copy(i, m - 1)
                    act.wait_ge(S["msg_made"], i * (2 * NQ) + (m + 1))
                    A.copy(msg[m % 2][:, :, 0:F], bank[5][:, 0:QW * F].rearrange("p (t f) -> p t f", f=F))\
                        .then_inc(S["msg_ready"], 1)
                sums_copy(i, 2 * NQ - 1)

            layer0_body(0, True)
            if EB > 1:
                with act.Fori(1, EB) as i:
                    layer0_body(i)

            with act.Fori(0, NCH // 2) as i:
                for b in range(2):
                    act.wait_ge(S["node_made"], i * 2 + (b + 1))
                    act.dma_start(node_rows(nodes, i * 2 + b), flat(g36[b])).then_inc(S[f"node_written{b}"], 16)

            act.wait_ge(S["keepc_set"], 1)
            for c in range(ECH):
                A.copy(keepx[:, c, :].rearrange("p (f j) -> p f j", j=CW),
                       cols(keepc, c).unsqueeze(1).to_broadcast([P, F, CW])).then_inc(S["keepx_set"], 1)
            act.wait_ge(S["roots_asked"], 1)
            A.activation(e1, e1, ACT.Sqrt).then_inc(S["roots_set"], 1)
            A.activation(e2, e2, ACT.Sqrt).then_inc(S["roots_set"], 1)

            def run_copy(q, i, b):
                act.wait_ge(S["scanned"], q * ECH + (i * 2 + (b + 1 - ECH)))
                act.wait_ge(S[f"run_written{b}"], q * (16 * EB) + (i * 16 + (1 - 16 * EB)))
                A.copy(ro[b], rf[b].rearrange("p f j -> p j f")).then_inc(S["run_copied"], 1)

            def turned_copy(st, n, two=False):
                act.wait_ge(S[f"v_turned_{st}"], n + 1)
                if two:
                    A.copy(vT[1], T1)
                    act.drain()
                A.copy(vT[0], T0).then_inc(S[f"v_copied_{st}"], 1)

            with act.Fori(0, EB) as i:
                for b in range(2):
                    act.wait_ge(S["roots_asked"], i * 2 + (b + 2))
                    A.activation(small[:, 0:3, :], small[:, 0:3, :], ACT.Sqrt).then_inc(S["roots_set"], 1)
                    layernorm("q1", i * 2 + b)
                    run_copy(1, i, b)
            with act.Fori(0, EB) as i:
                for b in range(2):
                    turned_copy("q2", i * 2 + b)
                    run_copy(2, i, b)
            with act.Fori(0, EB) as i:
                for b in range(2):
                    layernorm("q3", i * 2 + b)
                    run_copy(3, i, b)
            with act.Fori(0, EB) as i:
                for b in range(2):
                    turned_copy("q4", i * 2 + b, True)
                    layernorm("q4", i * 2 + b)
                    run_copy(4, i, b)

            def side_chunk(side, n):
                layernorm(side, n * 3)
                turned_copy(side, n * 2)
                layernorm(side, n * 3 + 1)
                turned_copy(side, n * 2 + 1, side == "d")
                layernorm(side, n * 3 + 2)

            def body(q0, q, i, n):
                if n is not None:
                    side_chunk("n", n)
                for b in range(2):
                    run_copy(q, i, b)

            layer3(act, lambda d, n: side_chunk("d", d), body)

        @block.tensor
        def _(pe):
            pe.wait_ge(S["disorder_counted"], 1)
            T.matmul(SETUP[:, 0:1], ones, disorder, start=True, stop=True).then_inc(S["disorder_summed"], 1)
            pe.wait_ge(S["iota_set"], 5)
            pe.wait_ge(S["w1t_set"], 1)
            T.transpose(SETUP[0:64, 0:F], w1s[0:F, :], ident[0:F, 0:F]).then_inc(S["w1_turned"], 1)
            pe.wait_ge(S["w1t_set"], 2)
            T.matmul(SETUP[0:F, 64:64 + F], w1t[0:64, :], w2s[0:64, :], start=True, stop=True)
            T.matmul(SETUP[:, 128:128 + F], b1b[0:64, :], w2s[0:64, :], start=True, stop=True).then_inc(S["w12_made"], 1)
            none = nil[:, 0:1].to_broadcast([P, HW])
            for k in range(2):
                T.matmul(bank[k][:, 0:HW], nil, none, start=True, stop=False)
            with pe.Fori(0, EB) as i:
                def turn_src(m):
                    b, n = divmod(m, NQ)
                    pe.wait_ge(S["srcc_set"], i * 2 + (b + 1))
                    pe.wait_ge(S["same_set"], i * (2 * NQ) + (m + 1))
                    for t in range(QW):
                        j = n * QW + t
                        last = T.transpose(bank[4][:, t * P:(t + 1) * P], srcc[b][:, j:j + 1].to_broadcast([P, P]), ident[:, :])
                    last.then_inc(S["src_turned"], 1)

                def turn_z(m, t):
                    pe.wait_ge(S["zT_copied"], i * (8 * NQ) + (4 * m + t + 1))
                    for k in range(4):
                        last = T.transpose(bank[2 + t % 2][:, k * P:(k + 1) * P],
                                           zz[m % 2][:, t].rearrange("p k f -> p (k f)")[:, k * P:(k + 1) * P], ident[:, :])
                    last.then_inc(S["z_turned"], 1)
                    return last

                def message(m, t):
                    pe.wait_ge(S["zT_copied"], i * (8 * NQ) + (4 * m + t + 3))
                    for k in range(4):
                        last = T.matmul(bank[5][:, t * F:(t + 1) * F], zT[t % 2][:, k * P:(k + 1) * P], w0r[:, k, :],
                                        start=(k == 0), stop=(k == 3))
                    return last

                def sum_src(m):
                    k = i * (2 * NQ) + m
                    pe.wait_ge(S["msg_ready"], k + 2)
                    pe.wait_ge(S["same_set"], k + 2)
                    pe.wait_ge(S["sums_copied"], k + 1)
                    for t in range(QW):
                        last = T.matmul(bank[6][:, t * TW:(t + 1) * TW], s4[m % 2][:, t, :], msg[m % 2][:, t, :],
                                        start=True, stop=True)
                    last.then_inc(S["sum_ready"], 1)

                for m in range(2 * NQ):
                    turn_src(m)
                    pe.wait_ge(S["z_ready"], i * (2 * NQ) + (m + 1))
                    turn_z(m, 0)
                    turn_z(m, 1)
                    if m:
                        sum_src(m - 1)
                    pe.wait_ge(S["msg_ready"], i * (2 * NQ) + (m + 1))
                    message(m, 0)
                    turn_z(m, 2)
                    message(m, 1)
                    turn_z(m, 3)
                    message(m, 2)
                    message(m, 3).then_inc(S["msg_made"], 1)
                    pe.sem_inc(S["z_used"], 1)
                    for t in range(QW):
                        pe.wait_ge(S["hot_ready"], i * (8 * NQ) + (4 * m + t + 1))
                        for h in range(2):
                            last = T.matmul(bank[h][:, 0:HW], hotp[:, t, :], hot[:, t, h * HW:(h + 1) * HW],
                                            start=False, stop=False)
                        last.then_inc(S["hot_used"], 1)
                sum_src(2 * NQ - 1)
            for k in range(2):
                last = T.matmul(bank[k][:, 0:HW], nil, none, start=False, stop=True)
            last.then_inc(S["hist_done"], 1)
            pe.wait_ge(S["tot_ready"], 1)
            T.matmul(SETUP[:, 0:NCH], after, ntot, start=True, stop=True)
            T.matmul(SETUP[:, NCH:2 * NCH], ones, ntot, start=True, stop=True).then_inc(S["offsets_made"], 1)

            pe.wait_ge(S["matrices_set"], 1)
            T.transpose(SETUP[:, 0:P], dstf[:, 0:1].to_broadcast([P, P]), ident[:, :]).then_inc(S["dst0_turned"], 1)
            pe.wait_ge(S["link_set"], 1)
            T.matmul(SETUP[:, 0:1], link[:, :], e2[:, EC - 1:EC], start=True, stop=True).then_inc(S["count_carry"], 1)

            def product(st, n, parts):
                pe.wait_ge(S[f"v_ready_{st}"], n + 1)
                for (v, _), tp in zip(parts, (T0, T1)):
                    for m in range(NQ):
                        last = T.transpose(tp[:, m * P:(m + 1) * P], flat(v)[:, m * P:(m + 1) * P], ident[:, :])
                last.then_inc(S[f"v_turned_{st}"], 1)
                pe.wait_ge(S[f"v_copied_{st}"], n + 1)
                for m in range(NQ):
                    for k, (_, w) in enumerate(parts):
                        last = T.matmul(U[:, m * P:(m + 1) * P], vT[k][:, m * P:(m + 1) * P], w[:, :],
                                        start=(k == 0), stop=(k == len(parts) - 1))
                last.then_inc(S[f"u_ready_{st}"], 1)

            def carry(q0, q):
                pe.wait_ge(S["ends_ready"], q)
                T.matmul(CARRY, link[:, :], ends[:, :], start=True, stop=True).then_inc(S["carry_ready"], 1)

            carry(1, 1)
            pe.wait_ge(S["bd_loaded"], 16 * QW)
            with pe.Fori(0, EB) as i:
                for b in range(2):
                    product("q2", i * 2 + b, [(ta, bd12)])
            carry(2, 2)
            carry(3, 3)
            with pe.Fori(0, EB) as i:
                for b in range(2):
                    product("q4", i * 2 + b, [(su, bda), (ta, bdb)])
            carry(4, 4)

            def one(half, q, k):
                nb, n0, m, d0 = plan(half)
                for t in range(m):
                    d = k * m + (d0 + t)
                    product("d", d * 2, [(ta, bd12)])
                    product("d", d * 2 + 1, [(su, bda), (ta, bdb)])
                if nb:
                    with pe.Fori(0, nb) as i:
                        n = k * nb + (n0 + i)
                        product("n", n * 2, [(su, bd12)])
                        product("n", n * 2 + 1, [(su, bda)])
                carry(None, q)

            for half in range(2):
                with pe.Fori(0, HALF) as k:
                    one(half, k + (Q0 + half * HALF), k)
            one(2, Q_LAST, 0)


_INS = ["x", "src", "dst", "edge_attr_2", "L0_gnn_weight", "L1_gnn_W1", "L1_gnn_b1", "L1_gnn_W2", "L1_gnn_b2",
        "L2_gnn_W", "L2_gnn_b"]


def kernel(**inputs):
    import numpy as np
    import concourse.bacc as bacc
    from concourse import mybir as mb
    from concourse.bass_utils import run_bass_kernel_spmd

    nc = bacc.Bacc("TRN2", target_bir_lowering=False, num_devices=1)
    arrays, args = {}, []
    for name in _INS:
        a = np.ascontiguousarray(inputs[name])
        arrays[f"in_{name}"] = a
        args.append(nc.dram_tensor(f"in_{name}", a.shape, mb.dt.from_np(a.dtype), kind="ExternalInput").ap())
    shape = arrays["in_x"].shape
    args.append(nc.dram_tensor("out_x", shape, mb.dt.float32, kind="ExternalOutput").ap())
    gnn_stack(nc, *args)
    return run_bass_kernel_spmd(nc, [arrays], core_ids=[0]).results[0]["out_x"]
```
